# Optimizing a Trainium2 kernel written in Bass

```python
import numpy as np
import jax
import jax.numpy as jnp

def _softmax(x, axis=-1):
    return jax.nn.softmax(x, axis=axis)

def _gelu(x):
    return jax.nn.gelu(x, approximate=True)

def _silu(x):
    return jax.nn.silu(x)

def _sigmoid(x):
    return jax.nn.sigmoid(x)

def _layernorm(x, axis=-1, eps=1e-05):
    m = jnp.mean(x, axis=axis, keepdims=True)
    v = jnp.var(x, axis=axis, keepdims=True)
    return (x - m) / jnp.sqrt(v + eps)

def _scatter_add(tgt, idx, src, axis=0):
    return tgt.at[idx].add(src)

def _segment_sum(src, seg, n):
    return jax.ops.segment_sum(src, seg, n)
kernel_name = 'mk_dlrm_tower_d1_rec_r8_58edbe'

def setup_inputs(seed: int=0):
    np.random.seed(seed)
    _w = jnp.asarray

    def _rec_inputs():
        import jax
        import jax.numpy as jnp
        _tk = jax.random.key(seed)
        dense_ctx = jax.random.normal(jax.random.fold_in(_tk, 190), (1024, 16), jnp.float32)
        ids = jnp.stack([jax.random.randint(jax.random.fold_in(_tk, 200 + f), (1024,), 0, v, jnp.int32) for f, v in enumerate([1000, 1000, 1000, 1250, 12500, 125000, 125000, 1250, 1000, 1250, 1250, 125000, 1000, 1000, 12500, 125000, 12500, 125000, 125000, 12500, 1250, 1000, 125000, 1000, 1000, 12500, 1250, 1000, 12500, 1000, 1000, 1000])], axis=1)
        tbl_0 = 0.05 * jax.random.normal(jax.random.fold_in(_tk, 500 + 0), (1000, 16), jnp.float32)
        tbl_1 = 0.05 * jax.random.normal(jax.random.fold_in(_tk, 500 + 1), (1000, 16), jnp.float32)
        tbl_2 = 0.05 * jax.random.normal(jax.random.fold_in(_tk, 500 + 2), (1000, 16), jnp.float32)
        tbl_3 = 0.05 * jax.random.normal(jax.random.fold_in(_tk, 500 + 3), (1250, 16), jnp.float32)
        tbl_4 = 0.05 * jax.random.normal(jax.random.fold_in(_tk, 500 + 4), (12500, 16), jnp.float32)
        tbl_5 = 0.05 * jax.random.normal(jax.random.fold_in(_tk, 500 + 5), (125000, 16), jnp.float32)
        tbl_6 = 0.05 * jax.random.normal(jax.random.fold_in(_tk, 500 + 6), (125000, 16), jnp.float32)
        tbl_7 = 0.05 * jax.random.normal(jax.random.fold_in(_tk, 500 + 7), (1250, 16), jnp.float32)
        tbl_8 = 0.05 * jax.random.normal(jax.random.fold_in(_tk, 500 + 8), (1000, 16), jnp.float32)
        tbl_9 = 0.05 * jax.random.normal(jax.random.fold_in(_tk, 500 + 9), (1250, 16), jnp.float32)
        tbl_10 = 0.05 * jax.random.normal(jax.random.fold_in(_tk, 500 + 10), (1250, 16), jnp.float32)
        tbl_11 = 0.05 * jax.random.normal(jax.random.fold_in(_tk, 500 + 11), (125000, 16), jnp.float32)
        tbl_12 = 0.05 * jax.random.normal(jax.random.fold_in(_tk, 500 + 12), (1000, 16), jnp.float32)
        tbl_13 = 0.05 * jax.random.normal(jax.random.fold_in(_tk, 500 + 13), (1000, 16), jnp.float32)
        tbl_14 = 0.05 * jax.random.normal(jax.random.fold_in(_tk, 500 + 14), (12500, 16), jnp.float32)
        tbl_15 = 0.05 * jax.random.normal(jax.random.fold_in(_tk, 500 + 15), (125000, 16), jnp.float32)
        tbl_16 = 0.05 * jax.random.normal(jax.random.fold_in(_tk, 500 + 16), (12500, 16), jnp.float32)
        tbl_17 = 0.05 * jax.random.normal(jax.random.fold_in(_tk, 500 + 17), (125000, 16), jnp.float32)
        tbl_18 = 0.05 * jax.random.normal(jax.random.fold_in(_tk, 500 + 18), (125000, 16), jnp.float32)
        tbl_19 = 0.05 * jax.random.normal(jax.random.fold_in(_tk, 500 + 19), (12500, 16), jnp.float32)
        tbl_20 = 0.05 * jax.random.normal(jax.random.fold_in(_tk, 500 + 20), (1250, 16), jnp.float32)
        tbl_21 = 0.05 * jax.random.normal(jax.random.fold_in(_tk, 500 + 21), (1000, 16), jnp.float32)
        tbl_22 = 0.05 * jax.random.normal(jax.random.fold_in(_tk, 500 + 22), (125000, 16), jnp.float32)
        tbl_23 = 0.05 * jax.random.normal(jax.random.fold_in(_tk, 500 + 23), (1000, 16), jnp.float32)
        tbl_24 = 0.05 * jax.random.normal(jax.random.fold_in(_tk, 500 + 24), (1000, 16), jnp.float32)
        tbl_25 = 0.05 * jax.random.normal(jax.random.fold_in(_tk, 500 + 25), (12500, 16), jnp.float32)
        tbl_26 = 0.05 * jax.random.normal(jax.random.fold_in(_tk, 500 + 26), (1250, 16), jnp.float32)
        tbl_27 = 0.05 * jax.random.normal(jax.random.fold_in(_tk, 500 + 27), (1000, 16), jnp.float32)
        tbl_28 = 0.05 * jax.random.normal(jax.random.fold_in(_tk, 500 + 28), (12500, 16), jnp.float32)
        tbl_29 = 0.05 * jax.random.normal(jax.random.fold_in(_tk, 500 + 29), (1000, 16), jnp.float32)
        tbl_30 = 0.05 * jax.random.normal(jax.random.fold_in(_tk, 500 + 30), (1000, 16), jnp.float32)
        tbl_31 = 0.05 * jax.random.normal(jax.random.fold_in(_tk, 500 + 31), (1000, 16), jnp.float32)
        _rk = jax.random.fold_in(_tk, 7)
        W_top1 = 0.0693375 * jax.random.normal(jax.random.fold_in(_tk, 801), (208, 512), jnp.float32)
        W_top2 = 0.0441942 * jax.random.normal(jax.random.fold_in(_tk, 802), (512, 256), jnp.float32)
        W_top3 = 0.0625 * jax.random.normal(jax.random.fold_in(_tk, 803), (256, 1), jnp.float32)
        b_top1 = jnp.zeros((512,), jnp.float32)
        b_top2 = jnp.zeros((256,), jnp.float32)
        return (dense_ctx, ids, tbl_0, tbl_1, tbl_2, tbl_3, tbl_4, tbl_5, tbl_6, tbl_7, tbl_8, tbl_9, tbl_10, tbl_11, tbl_12, tbl_13, tbl_14, tbl_15, tbl_16, tbl_17, tbl_18, tbl_19, tbl_20, tbl_21, tbl_22, tbl_23, tbl_24, tbl_25, tbl_26, tbl_27, tbl_28, tbl_29, tbl_30, tbl_31, W_top1, b_top1, W_top2, b_top2, W_top3)
    dense_ctx, ids, tbl_0, tbl_1, tbl_2, tbl_3, tbl_4, tbl_5, tbl_6, tbl_7, tbl_8, tbl_9, tbl_10, tbl_11, tbl_12, tbl_13, tbl_14, tbl_15, tbl_16, tbl_17, tbl_18, tbl_19, tbl_20, tbl_21, tbl_22, tbl_23, tbl_24, tbl_25, tbl_26, tbl_27, tbl_28, tbl_29, tbl_30, tbl_31, W_top1, b_top1, W_top2, b_top2, W_top3 = _rec_inputs()

    def _L0_rec_setup():
        import jax, jax.numpy as jnp
        import numpy as np
        B, M, D = (2048, 32, 16)
        LAYERS = [64, 64, 64]
        key = jax.random.key(seed)
        ks = jax.random.split(key, 4)
        inp = {'embeddings': jax.random.normal(ks[0], (B, M, D), dtype=jnp.float32)}
        hk_1 = M
        for i, hk in enumerate(LAYERS):
            scale = (2.0 / (M * hk_1 + hk)) ** 0.5
            inp[f'W{i}'] = jax.random.normal(ks[i + 1], (M, hk_1, hk), dtype=jnp.float32) * scale
            hk_1 = hk
        return inp
    _L0_rec_all = _L0_rec_setup()
    _L0_rec_in = {k: v for k, v in _L0_rec_all.items() if k in ('W0', 'W1', 'W2')}
    del _L0_rec_all
    return {'dense_ctx': dense_ctx, 'ids': ids, 'tbl_0': tbl_0, 'tbl_1': tbl_1, 'tbl_2': tbl_2, 'tbl_3': tbl_3, 'tbl_4': tbl_4, 'tbl_5': tbl_5, 'tbl_6': tbl_6, 'tbl_7': tbl_7, 'tbl_8': tbl_8, 'tbl_9': tbl_9, 'tbl_10': tbl_10, 'tbl_11': tbl_11, 'tbl_12': tbl_12, 'tbl_13': tbl_13, 'tbl_14': tbl_14, 'tbl_15': tbl_15, 'tbl_16': tbl_16, 'tbl_17': tbl_17, 'tbl_18': tbl_18, 'tbl_19': tbl_19, 'tbl_20': tbl_20, 'tbl_21': tbl_21, 'tbl_22': tbl_22, 'tbl_23': tbl_23, 'tbl_24': tbl_24, 'tbl_25': tbl_25, 'tbl_26': tbl_26, 'tbl_27': tbl_27, 'tbl_28': tbl_28, 'tbl_29': tbl_29, 'tbl_30': tbl_30, 'tbl_31': tbl_31, 'W_top1': W_top1, 'b_top1': b_top1, 'W_top2': W_top2, 'b_top2': b_top2, 'W_top3': W_top3, 'L0_rec_W0': _L0_rec_in['W0'], 'L0_rec_W1': _L0_rec_in['W1'], 'L0_rec_W2': _L0_rec_in['W2']}

def reference(dense_ctx, ids, tbl_0, tbl_1, tbl_2, tbl_3, tbl_4, tbl_5, tbl_6, tbl_7, tbl_8, tbl_9, tbl_10, tbl_11, tbl_12, tbl_13, tbl_14, tbl_15, tbl_16, tbl_17, tbl_18, tbl_19, tbl_20, tbl_21, tbl_22, tbl_23, tbl_24, tbl_25, tbl_26, tbl_27, tbl_28, tbl_29, tbl_30, tbl_31, W_top1, b_top1, W_top2, b_top2, W_top3, L0_rec_W0, L0_rec_W1, L0_rec_W2):
    import jax
    import jax.numpy as jnp

    def _L0_rec_ref(embeddings, W0, W1, W2):
        import jax, jax.numpy as jnp
        import numpy as np
        B, M, D = (2048, 32, 16)
        LAYERS = [64, 64, 64]
        x0 = embeddings
        xk = x0
        outs = []
        for W in (W0, W1, W2):
            xk = jax.nn.relu(jnp.einsum('bmd,bhd,mhk->bkd', x0, xk, W))
            outs.append(jnp.sum(xk, axis=2))
        return jnp.concatenate(outs, axis=1)
    e = jnp.stack([tbl_0[ids[:, 0]], tbl_1[ids[:, 1]], tbl_2[ids[:, 2]], tbl_3[ids[:, 3]], tbl_4[ids[:, 4]], tbl_5[ids[:, 5]], tbl_6[ids[:, 6]], tbl_7[ids[:, 7]], tbl_8[ids[:, 8]], tbl_9[ids[:, 9]], tbl_10[ids[:, 10]], tbl_11[ids[:, 11]], tbl_12[ids[:, 12]], tbl_13[ids[:, 13]], tbl_14[ids[:, 14]], tbl_15[ids[:, 15]], tbl_16[ids[:, 16]], tbl_17[ids[:, 17]], tbl_18[ids[:, 18]], tbl_19[ids[:, 19]], tbl_20[ids[:, 20]], tbl_21[ids[:, 21]], tbl_22[ids[:, 22]], tbl_23[ids[:, 23]], tbl_24[ids[:, 24]], tbl_25[ids[:, 25]], tbl_26[ids[:, 26]], tbl_27[ids[:, 27]], tbl_28[ids[:, 28]], tbl_29[ids[:, 29]], tbl_30[ids[:, 30]], tbl_31[ids[:, 31]]], axis=1)
    z = _L0_rec_ref(e, L0_rec_W0, L0_rec_W1, L0_rec_W2)
    z = z.reshape(z.shape[0], -1)
    h = jnp.concatenate([z, dense_ctx], axis=1)
    h = jnp.maximum(h @ W_top1 + b_top1, 0.0)
    h = jnp.maximum(h @ W_top2 + b_top2, 0.0)
    y = h @ W_top3
    return y

_drawn_inputs = setup_inputs


def setup_inputs(seed=0):
    import zlib

    import numpy as np

    out = dict(_drawn_inputs(seed))
    spreads = {'b_top1': (0.0, 2.0), 'b_top2': (0.0, 0.8)}
    factors = {'tbl_0': 8.0,
     'tbl_1': 8.0,
     'tbl_2': 8.0,
     'tbl_3': 8.0,
     'tbl_4': 8.0,
     'tbl_5': 8.0,
     'tbl_6': 8.0,
     'tbl_7': 8.0,
     'tbl_8': 8.0,
     'tbl_9': 8.0,
     'tbl_10': 8.0,
     'tbl_11': 8.0,
     'tbl_12': 8.0,
     'tbl_13': 8.0,
     'tbl_14': 8.0,
     'tbl_15': 8.0,
     'tbl_16': 8.0,
     'tbl_17': 8.0,
     'tbl_18': 8.0,
     'tbl_19': 8.0,
     'tbl_20': 8.0,
     'tbl_21': 8.0,
     'tbl_22': 8.0,
     'tbl_23': 8.0,
     'tbl_24': 8.0,
     'tbl_25': 8.0,
     'tbl_26': 8.0,
     'tbl_27': 8.0,
     'tbl_28': 8.0,
     'tbl_29': 8.0,
     'tbl_30': 8.0,
     'tbl_31': 8.0,
     'L0_rec_W0': 3.628,
     'L0_rec_W1': 8.0,
     'L0_rec_W2': 8.0,
     'dense_ctx': 7.79}
    for name, (base, spread) in spreads.items():
        noise = np.random.default_rng([zlib.crc32(name.encode()), seed]).standard_normal(out[name].shape)
        drawn = base * np.exp(spread * noise) if base else spread * noise
        out[name] = jnp.asarray(drawn.astype(out[name].dtype))
    for name, factor in factors.items():
        out[name] = (out[name] * factor).astype(out[name].dtype)
    return out
```

```python
import concourse.bass as bass
from concourse import mybir
from contextlib import ExitStack

B, M, D, K = 1024, 32, 16, 64
P = 128
CHUNKS = B // P
COLS = D * P
HALF = COLS // 2
BLK = HALF // 2
TILES = M * K // P
DMA_TILES = 4
PE_TILES = TILES - DMA_TILES
SHIFTS = 4
L1_TILES = M // 2 // SHIFTS + 1
L1_LAST = M // 2
SLOTS = 4
STEPS = TILES // 2
H1, H2 = 512, 256
QUART = COLS // 4

SPREADS = 2 * PE_TILES
HEAD = 14


def head(q):
    return {2 + j: [("spread", q, j)] for j in range(HEAD)}


def tail(q):
    return {j - HEAD: [("spread", q, j)] for j in range(HEAD, SPREADS)}


def with_next(at, extra):
    at = {k: list(v) for k, v in at.items()}
    for pos, job in extra:
        at.setdefault(pos, []).append(job)
    return at


AFTER = SPREADS - HEAD
PLAN = [tail(0),
        with_next(head(1), [(12, ("parts", 0)), (13, ("parts", 1)), (14, ("x0", 0)), (15, ("x0", 1))]),
        with_next(tail(1), [(AFTER, ("parts", 2)), (AFTER + 1, ("parts", 3)),
                            (AFTER + 2, ("x0", 2)), (AFTER + 3, ("x0", 3))]),
        head(0)]
PLAN_LAST = [tail(0), head(1), tail(1), {}]


def in_order(plan):
    return [job for at in plan for k in sorted(at) for job in at[k]]


JOBS = in_order(PLAN)
JOBS_LAST = in_order(PLAN_LAST)
JOBS_FIRST = [("parts", i) for i in range(4)] + [("x0", i) for i in range(4)] + \
             [("spread", 0, j) for j in range(HEAD)]
assert len(JOBS) % 2 == 0 and len(JOBS_FIRST) % 2 == 0


def build(nc, ids, tables, dense_t, ident, select, w0a, w0b, w1, w2, wt1, bt1, wt2, bt2, wt3, out):
    fp32, bf16, i32 = mybir.dt.float32, mybir.dt.bfloat16, mybir.dt.int32
    ALU = mybir.AluOpType
    ACT = mybir.ActivationFunctionType

    with ExitStack() as ctx:
        def sb(name, shape, dt=fp32):
            return ctx.enter_context(nc.sbuf_tensor(name, shape, dt))

        def ps(name, shape):
            return ctx.enter_context(nc.psum_tensor(name, shape, fp32))

        def sem(name):
            return ctx.enter_context(nc.semaphore(name))

        scratch = nc.dram_tensor("x0_scratch", (CHUNKS, 2 * M, COLS), fp32, kind="Internal").ap()

        ids_all = sb("ids_all", [P, CHUNKS + 1, M], i32)
        idx = sb("idx", [P, M], i32)
        rows = sb("rows", [P, M * D])
        rest = sb("rest", [P, M * D])
        parts = sb("parts", [P, 3, M * D], bf16)
        x0rep = sb("x0rep", [P, COLS])
        x0parts = sb("x0parts", [3 * M, COLS], bf16)
        x0shift = sb("x0shift", [P, L1_TILES, HALF])
        spread_dma = sb("spread_dma", [P, 2, DMA_TILES, HALF])
        spread_pe = sb("spread_pe", [P, PE_TILES, HALF])
        prod = sb("prod", [P, SLOTS, 2, HALF])
        prod1 = sb("prod1", [P, L1_TILES, HALF])
        w_1 = sb("w_1", [P, L1_TILES, K])
        w_1b = sb("w_1b", [P, L1_TILES, K])
        w_2 = sb("w_2", [P, TILES, K])
        w_3 = sb("w_3", [P, TILES, K])
        identb = sb("identb", [P, P], bf16)
        sel = sb("sel", [3 * M, PE_TILES + 1, P], bf16)
        relu_out = [sb(f"relu_out{l}", [P, BLK]) for l in range(3)]
        half_sum = sb("half_sum", [P, 2 * P])
        pair_sum = sb("pair_sum", [P, 3, P])
        last_sum = sb("last_sum", [P, P])
        z = sb("z", [P, 3, B])
        b_1 = sb("b_1", [P, H1 // P])
        b_2 = sb("b_2", [P, H2 // P])
        w_top3 = sb("w_top3", [P, H2 // P])
        y = x0rep[0:1, 0:B]
        old = spread_dma[:, 0, :, :].rearrange("p t n -> p (t n)")
        w_top1 = old[:, 0:3 * H1].rearrange("p (l n) -> p l n", l=3)
        w_topd = old[0:D, 3 * H1:4 * H1]
        w_top2 = old[:, 4 * H1:4 * H1 + H1 // P * H2].rearrange("p (t n) -> p t n", n=H2)
        dense = old[0:D, 4 * H1 + 1024:4 * H1 + 1024 + B]
        h_1 = [prod[:, 2 * i, :, :].rearrange("p a n -> p (a n)").rearrange("p (t n) -> p t n", n=BLK)
               for i in range(2)]
        h_2 = [prod[:, 2 * i + 1, 0, :].rearrange("p (t n) -> p t n", n=BLK) for i in range(2)]
        flat = prod[:, :, :, :].rearrange("p s a n -> p (s a n)")
        sel_f32 = flat[0:3 * M, 0:(PE_TILES + 1) * P]
        identf = flat[:, (PE_TILES + 1) * P:(PE_TILES + 2) * P]

        acc = [ps(f"acc{i}", [P, BLK]) for i in range(2)]
        staged = [ps(f"staged{i}", [P, BLK]) for i in range(2)]
        x1 = ps("x1", [P, HALF])
        x2 = ps("x2", [P, HALF])

        ids_in = sem("ids_in")
        consts_in = sem("consts_in")
        w1_in = sem("w1_in")
        w23_in = sem("w23_in")
        small_in = sem("small_in")
        tower_in = sem("tower_in")
        ids_padded = sem("ids_padded")
        idx_set = sem("idx_set")
        gathered = sem("gathered")
        split = sem("split")
        cast_done = sem("cast_done")
        w1_zeroed = sem("w1_zeroed")
        w1_folded = sem("w1_folded")
        filled = sem("filled")
        emptied = sem("emptied")
        scratch_in = [sem(f"scratch_in{i}") for i in range(2)]
        shift_in = sem("shift_in")
        spread_in = [sem(f"spread_in{i}") for i in range(2)]
        prod1_ready = sem("prod1_ready")
        prod1_free = sem("prod1_free")
        prod_ready = sem("prod_ready")
        prod_free = sem("prod_free")
        x1_ready = sem("x1_ready")
        x2_ready = sem("x2_ready")
        relu_ready = [sem(f"relu_ready{l}") for l in range(3)]
        relu_free = [sem(f"relu_free{l}") for l in range(3)]
        summed = sem("summed")
        passed = sem("passed")
        h1_mm, h1_out, h2_mm, h2_out = sem("h1_mm"), sem("h1_out"), sem("h2_mm"), sem("h2_out")
        y_mm, y_out, stored = sem("y_mm"), sem("y_out"), sem("stored")

        def job_no(c, job, jobs=JOBS):
            return len(JOBS_FIRST) + len(JOBS) * c + jobs.index(job)

        def spread_done(c, q, i, jobs):
            j = 2 * i + 1
            if q == 0 and j < HEAD:
                if isinstance(c, int) and c == 0:
                    return 2 + JOBS_FIRST.index(("spread", 0, j)) + 1
                return 2 + len(JOBS_FIRST) + len(JOBS) * (c - 1) + JOBS.index(("spread", 0, j)) + 1
            return 2 + job_no(c, ("spread", q, j), jobs) + 1

        def x0parts_done(c, i):
            if isinstance(c, int) and c == 0:
                return 2 + JOBS_FIRST.index(("parts", i)) + 1
            return 2 + job_no(c - 1, ("parts", i)) + 1

        FIRST_SUMS, SUMS = 1, 9

        block = ctx.enter_context(nc.Block())

        @block.sync
        def _(sp):
            def held(semaphore, value):
                sp.wait_ge(semaphore, value)
                sp.sem_inc(passed, 1)

            sp.dma_start(ids_all[:, 0:CHUNKS, :], ids.rearrange("(c p) m -> p c m", p=P)).then_inc(ids_in, 16)
            sp.dma_start(identf, ident).then_inc(consts_in, 16)
            sp.dma_start(sel_f32.rearrange("p (t n) -> p t n", n=P),
                         select[:, DMA_TILES:TILES + 1, :]).then_inc(consts_in, 16)
            sp.dma_start(w_1[:, 0:4, :], w0a[:, 0:4, :]).then_inc(w1_in, 16)
            sp.dma_start(w_1[0:L1_LAST, 4, :], w0a[0:L1_LAST, 4, :]).then_inc(w1_in, 16)
            sp.wait_ge(w1_zeroed, 1)
            sp.dma_start(w_1b[M:P, 0, :], w0b[M:P, 0, :]).then_inc(w1_in, 16)
            sp.dma_start(w_1b[:, 1:4, :], w0b[:, 1:4, :]).then_inc(w1_in, 16)
            sp.dma_start(w_1b[0:L1_LAST, 4, :], w0b[0:L1_LAST, 4, :]).then_inc(w1_in, 16)
            for w_sb, w_dram in ((w_2, w1), (w_3, w2)):
                for a in range(2):
                    sp.dma_start(w_sb[K * a:K * a + K, :, :],
                                 w_dram.rearrange("(t a) h k -> a h t k", a=2)[a]).then_inc(w23_in, 16)
            sp.dma_start(b_1[:, :], bt1.rearrange("(t p) -> p t", p=P), allow_slow_non_contiguous=True).then_inc(small_in, 16)
            sp.dma_start(b_2[:, :], bt2.rearrange("(t p) -> p t", p=P), allow_slow_non_contiguous=True).then_inc(small_in, 16)
            sp.dma_start(w_top3[:, :], wt3.rearrange("(t p) o -> p (t o)", p=P), allow_slow_non_contiguous=True).then_inc(small_in, 16)

            def store_x0(c, q, done):
                held(emptied, done)
                sp.dma_start(scratch[c, :, q * HALF:(q + 1) * HALF],
                             x0rep[0:2 * M, q * HALF:(q + 1) * HALF]).then_inc(scratch_in[q], 16)

            def load_shifts(c, q, pair):
                held(scratch_in[q], 16 * (c + 1))
                if not (isinstance(pair, int) and pair == 0):
                    held(prod1_ready, L1_TILES * pair)
                for g in range(SHIFTS):
                    at = scratch[c, g, q * HALF:(q + 1) * HALF]
                    src = bass.AP(tensor=at.tensor, offset=at.offset,
                                  ap=[[COLS, M], [SHIFTS * COLS, 4], [1, HALF]])
                    sp.dma_start(x0shift[M * g:M * g + M, 0:4, :], src).then_inc(shift_in, 16)
                sp.dma_start(x0shift[0:L1_LAST, 4, :],
                             scratch[c, M // 2:M // 2 + L1_LAST, q * HALF:(q + 1) * HALF]).then_inc(shift_in, 16)

            def load_spread(c, q, used):
                held(scratch_in[q], 16 * (c + 1))
                if used is not None:
                    held(prod_ready, used)
                for a in range(2):
                    at = scratch[c, a, q * HALF:(q + 1) * HALF]
                    src = bass.AP(tensor=at.tensor, offset=at.offset,
                                  ap=[[0, K], [2 * COLS, DMA_TILES], [1, HALF]])
                    sp.dma_start(spread_dma[K * a:K * a + K, q, :, :], src).then_inc(spread_in[q], 16)

            store_x0(0, 0, 2 + 6)
            load_shifts(0, 0, 0)
            store_x0(0, 1, 2 + 8)
            load_spread(0, 0, None)
            load_shifts(0, 1, 1)
            load_spread(0, 1, None)
            with sp.Fori(0, CHUNKS - 1) as c:
                store_x0(c + 1, 0, 2 + job_no(c, ("x0", 1)) + 1)
                load_shifts(c + 1, 0, 2 * c + 2)
                store_x0(c + 1, 1, 2 + job_no(c, ("x0", 3)) + 1)
                load_spread(c + 1, 0, 4 * STEPS * c + 2 * STEPS)
                load_shifts(c + 1, 1, 2 * c + 3)
                load_spread(c + 1, 1, 4 * STEPS * c + 4 * STEPS)
            sp.wait_ge(prod_ready, 4 * STEPS * (CHUNKS - 1) + 2 * STEPS)
            for a in range(2):
                sp.dma_start(w_top1[K * a:K * a + K, :, :],
                             wt1[0:3 * K, :].rearrange("(l p) n -> p l n", p=K)).then_inc(tower_in, 16)
            sp.dma_start(w_topd, wt1[3 * K:3 * K + D, :]).then_inc(tower_in, 16)
            sp.dma_start(w_top2, wt2.rearrange("(t p) n -> p t n", p=P)).then_inc(tower_in, 16)
            sp.dma_start(dense, dense_t).then_inc(tower_in, 16)
            sp.wait_ge(y_out, 2)
            sp.dma_start(out.rearrange("b o -> o b"), y[:, :]).then_inc(stored, 16)
            sp.wait_ge(stored, 16)

        @block.gpsimd
        def _(pool):
            def held(semaphore, value):
                pool.wait_ge(semaphore, value)
                pool.sem_inc(passed, 1)

            def set_idx(c):
                nc.gpsimd.tensor_copy(idx[:, :], ids_all[:, c, :]).then_inc(idx_set, 1)

            def gather(fields):
                for m in fields:
                    nc.gpsimd.indirect_dma_start(
                        rows[:, m * D:(m + 1) * D], None, tables[m],
                        bass.IndirectOffsetOnAxis(ap=idx[:, m:m + 1], axis=0)).then_inc(gathered, 16)

            def split_rows(c, parts_read=0, first=False):
                held(gathered, 16 * M * (c + 1))
                if not first:
                    held(filled, parts_read)
                nc.gpsimd.tensor_copy(parts[:, 0, :], rows[:, :]).then_inc(split, 1)
                pool.wait_ge(split, 4 * c + 1)
                nc.gpsimd.tensor_tensor(rest[:, :], rows[:, :], parts[:, 0, :], ALU.subtract).then_inc(split, 1)
                held(split, 4 * c + 2)
                nc.gpsimd.tensor_copy(parts[:, 1, :], rest[:, :]).then_inc(split, 1)
                pool.wait_ge(split, 4 * c + 3)
                nc.gpsimd.tensor_tensor(parts[:, 2, :], rest[:, :], parts[:, 1, :], ALU.subtract).then_inc(split, 1)

            def layer_1(c, q, x0_done):
                pair = 2 * c + q
                pool.wait_ge(emptied, x0_done)
                pool.wait_ge(shift_in, 16 * (SHIFTS + 1) * (pair + 1))
                for j in range(L1_TILES):
                    n = P if j < L1_TILES - 1 else L1_LAST
                    pool.wait_ge(prod1_free, L1_TILES * pair + j + 1)
                    nc.gpsimd.tensor_tensor(prod1[0:n, j, :], x0rep[0:n, q * HALF:(q + 1) * HALF],
                                            x0shift[0:n, j, :], ALU.mult).then_inc(prod1_ready, 1)

            def sum_d(c, q, layer, so_far):
                r = relu_out[layer]
                pair = 2 * c + q
                pool.wait_ge(summed, so_far)
                pool.wait_ge(relu_ready[layer], pair + (2 if layer == 2 else 1))
                nc.gpsimd.tensor_tensor(half_sum[:, :], r[:, 0:2 * P], r[:, 2 * P:4 * P],
                                        ALU.add).then_inc(relu_free[layer], 1)
                pool.wait_ge(relu_free[layer], pair + 2)
                to = pair_sum[:, layer, :] if q == 0 else last_sum[:, :]
                nc.gpsimd.tensor_tensor(to, half_sum[:, 0:P], half_sum[:, P:2 * P], ALU.add).then_inc(summed, 1)
                if q == 1:
                    held(summed, so_far + 1)
                    nc.gpsimd.tensor_tensor(z[:, layer, bass.ts(c, P)], pair_sum[:, layer, :],
                                            last_sum[:, :], ALU.add).then_inc(summed, 1)

            pool.sem_inc(relu_free[0], 1)
            pool.sem_inc(relu_free[1], 1)
            pool.sem_inc(relu_free[2], 1)
            nc.gpsimd.memset(ids_all[:, CHUNKS, :], 0).then_inc(ids_padded, 1)
            pool.wait_ge(ids_padded, 1)
            pool.wait_ge(ids_in, 16)
            set_idx(0)
            pool.wait_ge(idx_set, 1)
            gather(range(M))
            split_rows(0, first=True)
            set_idx(1)
            pool.wait_ge(idx_set, 2)
            pool.wait_ge(split, 4)
            gather(range(M // 2))
            layer_1(0, 0, 2 + 6)
            sum_d(0, 0, 0, 0)

            def chunk(c, last):
                sums = FIRST_SUMS + SUMS * c
                x0_done = 2 + 8 if isinstance(c, int) and c == 0 else \
                    2 + len(JOBS_FIRST) + len(JOBS) * (c - 1) + JOBS.index(("x0", 3)) + 1
                layer_1(c, 1, x0_done)
                if not last:
                    gather(range(M // 2, M))
                sum_d(c, 0, 1, sums)
                sum_d(c, 1, 0, sums + 1)
                if not last:
                    split_rows(c + 1, parts_read=len(JOBS_FIRST) + len(JOBS) * c)
                sum_d(c, 0, 2, sums + 3)
                if not last:
                    layer_1(c + 1, 0, 2 + job_no(c, ("x0", 1)) + 1)
                    set_idx(c + 2)
                    held(idx_set, c + 3)
                    held(split, 4 * (c + 2))
                    gather(range(M // 2))
                sum_d(c, 1, 1, sums + 4)
                if not last:
                    sum_d(c + 1, 0, 0, sums + 6)
                    sum_d(c, 1, 2, sums + 7)
                else:
                    sum_d(c, 1, 2, sums + 6)

            with pool.Fori(0, CHUNKS - 1) as c:
                chunk(c, False)
            chunk(CHUNKS - 1, True)
            pool.wait_ge(gathered, 16 * (M * CHUNKS + M // 2))

        @block.vector
        def _(dve):
            nc.vector.memset(w_1b[0:M, 0, :], 0.0).then_inc(w1_zeroed, 1)
            dve.wait_ge(consts_in, 32)
            nc.vector.tensor_copy(identb[:, :], identf).then_inc(cast_done, 1)
            nc.vector.tensor_copy(sel[:, :, :].rearrange("p t n -> p (t n)"), sel_f32).then_inc(cast_done, 1)
            dve.wait_ge(w1_in, 80)
            dve.wait_ge(w1_zeroed, 1)
            nc.vector.tensor_tensor(w_1[:, 0:4, :], w_1[:, 0:4, :], w_1b[:, 0:4, :], ALU.add).then_inc(w1_folded, 1)
            nc.vector.tensor_tensor(w_1[0:L1_LAST, 4, :], w_1[0:L1_LAST, 4, :], w_1b[0:L1_LAST, 4, :],
                                    ALU.add).then_inc(w1_folded, 1)
            dve.wait_ge(cast_done, 2)

            def products(c, n, slot, x, spread):
                dve.wait_ge(prod_free, n + 1)
                nc.vector.tensor_tensor(prod[:, slot, :, :], spread,
                                        x[:, :].rearrange("p (a n) -> p a n", a=1).to_broadcast([P, 2, HALF]),
                                        ALU.mult).then_inc(prod_ready, 1)

            def spread_of(q, t):
                return spread_dma[:, q, t:t + 2, :] if t < DMA_TILES else \
                    spread_pe[:, t - DMA_TILES:t - DMA_TILES + 2, :]

            def chunk(c, jobs, first):
                for q in range(2):
                    n = 4 * STEPS * c + 2 * STEPS * q
                    dve.wait_ge(x1_ready, 2 * c + q + 1)
                    dve.wait_ge(spread_in[q], 32 * (c + 1))
                    for s in range(STEPS):
                        t = 2 * s
                        if t >= DMA_TILES:
                            dve.wait_ge(emptied, spread_done(c, q, t - DMA_TILES + 1, jobs))
                        products(c, n + s, s % SLOTS, x1, spread_of(q, t))
                    dve.wait_ge(x2_ready, 2 * c + q + 1)
                    for s in range(STEPS):
                        t = (2 * s + DMA_TILES) % TILES
                        products(c, n + STEPS + s, s % SLOTS, x2, spread_of(q, t))

            with dve.Fori(0, CHUNKS - 1) as c:
                chunk(c, JOBS, False)
            chunk(CHUNKS - 1, JOBS_LAST, False)

        @block.scalar
        def _(act):
            act.sem_inc(emptied, 2)
            act.sem_inc(relu_ready[2], 1)

            def empty(c, n, job):
                src = staged[n[1] % 2]
                act.wait_ge(filled, n[0] + n[1] + 1)
                if job[0] == "spread":
                    _, q, j = job
                    nc.scalar.activation(spread_pe[:, j // 2, (j % 2) * BLK:(j % 2 + 1) * BLK], src[:, :],
                                         ACT.Copy).then_inc(emptied, 1)
                elif job[0] == "x0":
                    i = job[1]
                    nc.scalar.activation(x0rep[:, i * QUART:(i + 1) * QUART], src[:, :],
                                         ACT.Copy).then_inc(emptied, 1)
                else:
                    i = job[1]
                    nc.scalar.activation(x0parts[:, i * QUART:(i + 1) * QUART],
                                         src[0:3 * M, 0:QUART // 2].bitcast(bf16), ACT.Copy).then_inc(emptied, 1)

            def twice(bank, to, ready, layer, pair):
                for blk in range(2):
                    for half in range(2):
                        last = nc.scalar.activation(to[K * half:K * half + K, blk * BLK:(blk + 1) * BLK],
                                                    acc[bank][K * blk:K * blk + K, :], ACT.Relu)
                last.then_inc(ready, 1)
                once(bank, layer, pair)

            def once(bank, layer, pair):
                act.wait_ge(relu_free[layer], pair + 1)
                nc.scalar.activation(relu_out[layer][:, :], acc[bank][:, :], ACT.Relu).then_inc(relu_ready[layer], 1)

            def contracted(c, stage):
                act.wait_ge(prod_free, SLOTS + 4 * STEPS * c + STEPS * (stage + 1))

            def contracted_1(pair):
                act.wait_ge(prod1_free, L1_TILES * (pair + 2))

            for n, job in enumerate(JOBS_FIRST):
                empty(0, (0, n), job)
            contracted_1(0)
            twice(1, x1, x1_ready, 0, 0)

            def chunk(c, plan, last):
                base, k = len(JOBS_FIRST) + len(JOBS) * c, 0

                def stage_jobs(at):
                    nonlocal k
                    for pos in sorted(at):
                        for job in at[pos]:
                            if job in (("x0", 0), ("x0", 2)):
                                q = job[1] // 2
                                act.wait_ge(prod1_ready, L1_TILES * (2 * c + q + 1))
                                act.wait_ge(scratch_in[q], 16 * (c + 1))
                            empty(c, (base, k), job)
                            k += 1

                stage_jobs(plan[0])
                contracted(c, 0)
                twice(0, x2, x2_ready, 1, 2 * c)
                contracted_1(2 * c + 1)
                twice(1, x1, x1_ready, 0, 2 * c + 1)
                stage_jobs(plan[1])
                contracted(c, 1)
                once(0, 2, 2 * c)
                stage_jobs(plan[2])
                contracted(c, 2)
                twice(1, x2, x2_ready, 1, 2 * c + 1)
                if not last:
                    contracted_1(2 * c + 2)
                    twice(0, x1, x1_ready, 0, 2 * c + 2)
                stage_jobs(plan[3])
                contracted(c, 3)
                once(0 if last else 1, 2, 2 * c + 1)

            with act.Fori(0, CHUNKS - 1) as c:
                chunk(c, PLAN, False)
            chunk(CHUNKS - 1, PLAN_LAST, True)

            act.wait_ge(small_in, 48)
            for i in range(2):
                act.wait_ge(h1_mm, i + 1)
                for t in range(H1 // P):
                    last = nc.scalar.activation(h_1[i][:, t, :], (x1, x2)[t // 2][:, (t % 2) * BLK:(t % 2 + 1) * BLK],
                                                ACT.Relu, bias=b_1[:, t:t + 1])
                last.then_inc(h1_out, 1)
                act.wait_ge(h2_mm, i + 1)
                for t in range(H2 // P):
                    last = nc.scalar.activation(h_2[i][:, t, :], acc[t][:, :], ACT.Relu, bias=b_2[:, t:t + 1])
                last.then_inc(h2_out, 1)
                act.wait_ge(y_mm, i + 1)
                nc.scalar.activation(y[:, i * BLK:(i + 1) * BLK], staged[i][0:1, :], ACT.Copy).then_inc(y_out, 1)

        @block.tensor
        def _(pe):
            pe.sem_inc(prod1_free, L1_TILES)
            pe.sem_inc(prod_free, SLOTS)

            def job_matmuls(c, n, job):
                to = staged[n[1] % 2]
                if job == ("parts", 0):
                    pe.wait_ge(split, 4 * (c + 1))
                if job[0] == "x0":
                    pe.wait_ge(emptied, x0parts_done(c, job[1]))
                pe.wait_ge(emptied, n[0] + n[1] + 1)
                if job[0] == "spread":
                    _, q, j = job
                    col = q * HALF + (j % 2) * BLK
                    nc.tensor.matmul(to[:, :], sel[:, j // 2, :], x0parts[:, col:col + BLK],
                                     start=True, stop=True).then_inc(filled, 1)
                elif job[0] == "x0":
                    nc.tensor.matmul(to[:, :], sel[:, PE_TILES, :], x0parts[:, job[1] * QUART:(job[1] + 1) * QUART],
                                     start=True, stop=True).then_inc(filled, 1)
                else:
                    for i in range(4):
                        d = 4 * job[1] + i
                        src = parts[:, 0, d:d + 1]
                        three = bass.AP(tensor=src.tensor, offset=src.offset,
                                        ap=[list(src.ap[0]), [D, 3 * M]])
                        last = nc.tensor.transpose(to[0:3 * M, i * P // 2:(i + 1) * P // 2].bitcast(bf16), three,
                                                   identb[:, :])
                    last.then_inc(filled, 1)

            def contract(bank, w, moving, start, stop):
                for blk in range(2):
                    last = nc.tensor.matmul(acc[bank][K * blk:K * blk + K, :], w,
                                            moving[:, blk * BLK:(blk + 1) * BLK], start=start, stop=stop)
                return last

            def layer_1(c, q, bank):
                for j in range(L1_TILES):
                    n = P if j < L1_TILES - 1 else L1_LAST
                    pe.wait_ge(prod1_ready, L1_TILES * (2 * c + q) + j + 1)
                    contract(bank, w_1[0:n, j, :], prod1[0:n, j, :], j == 0,
                             j == L1_TILES - 1).then_inc(prod1_free, 1)

            def layer(c, n, bank, w, first_tile, at, base, k):
                for i in range(TILES):
                    if i % 2 == 0:
                        pe.wait_ge(prod_ready, n + i // 2 + 1)
                    t = (i + first_tile) % TILES
                    last = contract(bank, w[:, t, :], prod[:, i // 2 % SLOTS, i % 2, :], i == 0, i == TILES - 1)
                    if i % 2 == 1:
                        last.then_inc(prod_free, 1)
                    for job in at.get(i, ()):
                        job_matmuls(c + 1, (base, k), job)
                        k += 1
                return k

            pe.wait_ge(consts_in, 32)
            pe.wait_ge(cast_done, 2)
            for n, job in enumerate(JOBS_FIRST):
                job_matmuls(0, (0, n), job)
            pe.wait_ge(w1_folded, 2)
            layer_1(0, 0, 1)
            pe.wait_ge(w23_in, 64)

            def chunk(c, plan, last):
                base = len(JOBS_FIRST) + len(JOBS) * c
                n = 4 * STEPS * c
                pe.wait_ge(relu_ready[0], 2 * c + 1)
                k = layer(c, n, 0, w_2, 0, plan[0], base, 0)
                pe.wait_ge(relu_ready[2], 2 * c + 1)
                layer_1(c, 1, 1)
                pe.wait_ge(relu_ready[1], 2 * c + 1)
                k = layer(c, n + STEPS, 0, w_3, DMA_TILES, plan[1], base, k)
                pe.wait_ge(relu_ready[0], 2 * c + 2)
                k = layer(c, n + 2 * STEPS, 1, w_2, 0, plan[2], base, k)
                pe.wait_ge(relu_ready[2], 2 * c + 2)
                if not last:
                    layer_1(c + 1, 0, 0)
                    pe.wait_ge(emptied, x0parts_done(c + 1, 3))
                    pe.wait_ge(relu_ready[1], 2 * c + 2)
                layer(c, n + 3 * STEPS, 0 if last else 1, w_3, DMA_TILES, plan[3], base, k)

            with pe.Fori(0, CHUNKS - 1) as c:
                chunk(c, PLAN, False)
            chunk(CHUNKS - 1, PLAN_LAST, True)

            pe.wait_ge(tower_in, 80)
            pe.wait_ge(small_in, 48)
            pe.wait_ge(summed, FIRST_SUMS + SUMS * CHUNKS - 1)
            for i in range(2):
                if i:
                    pe.wait_ge(h1_out, i)
                cols = slice(i * BLK, (i + 1) * BLK)
                for t in range(H1 // P):
                    to = (x1, x2)[t // 2][:, (t % 2) * BLK:(t % 2 + 1) * BLK]
                    for l in range(3):
                        nc.tensor.matmul(to, w_top1[:, l, t * P:(t + 1) * P], z[:, l, cols],
                                         start=l == 0, stop=False)
                    last = nc.tensor.matmul(to, w_topd[:, t * P:(t + 1) * P], dense[:, cols], start=False, stop=True)
                last.then_inc(h1_mm, 1)
                pe.wait_ge(h1_out, i + 1)
                if i:
                    pe.wait_ge(h2_out, i)
                for t in range(H2 // P):
                    for s in range(H1 // P):
                        last = nc.tensor.matmul(acc[t][:, :], w_top2[:, s, t * P:(t + 1) * P], h_1[i][:, s, :],
                                                start=s == 0, stop=s == H1 // P - 1)
                last.then_inc(h2_mm, 1)
                pe.wait_ge(h2_out, i + 1)
                for s in range(H2 // P):
                    last = nc.tensor.matmul(staged[i][0:1, :], w_top3[:, s:s + 1], h_2[i][:, s, :],
                                            start=s == 0, stop=s == H2 // P - 1)
                last.then_inc(y_mm, 1)


def kernel(**inputs):
    import numpy as np
    import concourse.bacc as bacc
    from concourse.bass_utils import run_bass_kernel_spmd

    nc = bacc.Bacc("TRN2", target_bir_lowering=False, num_devices=1)
    arrays = {}

    def give(name, a):
        arrays[name] = np.ascontiguousarray(a)
        return nc.dram_tensor(name, arrays[name].shape, mybir.dt.from_np(arrays[name].dtype),
                              kind="ExternalInput").ap()

    w0 = np.asarray(inputs["L0_rec_W0"])
    g, m, j = np.meshgrid(np.arange(SHIFTS), np.arange(M), np.arange(L1_TILES), indexing="ij")
    h = (m + SHIFTS * j + g) % M
    select = np.zeros((3, M, TILES + 1, 2, K), np.float32)
    for f in range(M):
        select[:, f, f // 2, f % 2, :] = 1.0
    select[:, :, TILES] = np.tile(np.eye(M, dtype=np.float32), (1, P // M)).reshape(M, 2, K)

    args = [give("ids", inputs["ids"]),
            [give(f"tbl_{i}", inputs[f"tbl_{i}"]) for i in range(M)],
            give("dense_t", np.asarray(inputs["dense_ctx"]).T),
            give("ident", np.eye(P, dtype=np.float32)),
            give("select", select.reshape(3 * M, TILES + 1, P)),
            give("w0a", w0[m, h].reshape(P, L1_TILES, K)),
            give("w0b", w0[h, m].reshape(P, L1_TILES, K)),
            give("w1", inputs["L0_rec_W1"]), give("w2", inputs["L0_rec_W2"]),
            give("wt1", inputs["W_top1"]), give("bt1", inputs["b_top1"]),
            give("wt2", inputs["W_top2"]), give("bt2", inputs["b_top2"]),
            give("wt3", inputs["W_top3"])]
    out = nc.dram_tensor("y_out_dram", (B, 1), mybir.dt.float32, kind="ExternalOutput").ap()
    build(nc, *args, out)
    r = run_bass_kernel_spmd(nc, [arrays], core_ids=[0])
    return r.results[0]["y_out_dram"]
```

```python
import concourse.bass as bass
from concourse import mybir
from contextlib import ExitStack

B, M, D, K = 1024, 32, 16, 64
P = 128
CHUNKS = B // P
COLS = D * P
HALF = COLS // 2
BLK = HALF // 2
TILES = M * K // P
STEPS = TILES // 2
DMA_STEPS = (0, 2, 4, 6)
EARLY_STEPS = tuple(s for s in DMA_STEPS if s < 6)
LATE_STEPS = tuple(s for s in DMA_STEPS if s >= 6)
PE_STEPS = tuple(s for s in range(STEPS) if s not in DMA_STEPS)
SHIFTS = 4
L1_TILES = M // 2 // SHIFTS + 1
L1_LAST = M // 2
SLOTS = 4
H1, H2 = 512, 256
QUART = COLS // 4
SOON, NEXT = 14, 8

SPREADS = 4 * len(PE_STEPS)


def spread_times():
    times = []
    for j in range(SPREADS):
        s = PE_STEPS[j // 4]
        at = max([2 * s + 3] + [t + 1 for t in times[-1:]])
        assert at <= 16 + 2 * s - 2
        times.append(at)
    return times


TIMES = spread_times()
HEAD = sum(t < TILES for t in TIMES)


def head(q):
    return {TIMES[j]: [("spread", q, j)] for j in range(HEAD)}


def tail(q):
    return {TIMES[j] - TILES: [("spread", q, j)] for j in range(HEAD, SPREADS)}


def spread_at(j):
    return 2 * PE_STEPS[j // 4] + j % 4 // 2, j % 2


def with_next(at, extra):
    at = {k: list(v) for k, v in at.items()}
    for pos, job in extra:
        at.setdefault(pos, []).append(job)
    return at


AFTER = max([TIMES[j] - TILES for j in range(HEAD, SPREADS)], default=-1) + 1
PLAN = [tail(0),
        with_next(head(1), [(5, ("parts", 0)), (6, ("parts", 1)), (7, ("x0", 0)), (8, ("x0", 1))]),
        with_next(tail(1), [(AFTER, ("parts", 2)), (AFTER + 1, ("parts", 3)),
                            (AFTER + 2, ("x0", 2)), (AFTER + 3, ("x0", 3))]),
        head(0)]
PLAN_LAST = [tail(0), head(1), tail(1), {}]


def in_order(plan):
    return [job for at in plan for k in sorted(at) for job in at[k]]


JOBS = in_order(PLAN)
JOBS_LAST = in_order(PLAN_LAST)
JOBS_FIRST = [("parts", i) for i in range(4)] + [("x0", i) for i in range(4)] + \
             [("spread", 0, j) for j in range(HEAD)]
assert len(JOBS) % 2 == 0


def build(nc, ids, tables, dense_t, ident, select, w0a, w0b, w1, w2, wt1, bt1, wt2, bt2, wt3, out):
    fp32, bf16, i32 = mybir.dt.float32, mybir.dt.bfloat16, mybir.dt.int32
    ALU = mybir.AluOpType
    ACT = mybir.ActivationFunctionType

    with ExitStack() as ctx:
        def sb(name, shape, dt=fp32):
            return ctx.enter_context(nc.sbuf_tensor(name, shape, dt))

        def ps(name, shape):
            return ctx.enter_context(nc.psum_tensor(name, shape, fp32))

        def sem(name):
            return ctx.enter_context(nc.semaphore(name))

        scratch = nc.dram_tensor("x0_scratch", (CHUNKS, 2 * M, COLS), fp32, kind="Internal").ap()

        ids_all = sb("ids_all", [P, CHUNKS + 1, M], i32)
        idx = sb("idx", [P, M], i32)
        rows = sb("rows", [P, M * D])
        rest = sb("rest", [P, M * D])
        parts = sb("parts", [P, 3, M * D], bf16)
        x0rep = sb("x0rep", [P, COLS])
        x0parts = sb("x0parts", [3 * M, COLS], bf16)
        x0shift = sb("x0shift", [P, L1_TILES, HALF])
        spread = sb("spread", [P, TILES, HALF])
        prod = sb("prod", [P, SLOTS, 2, HALF])
        prod1 = sb("prod1", [P, L1_TILES, HALF])
        w_1 = sb("w_1", [P, L1_TILES, K])
        w_1b = sb("w_1b", [P, L1_TILES, K])
        w_2 = sb("w_2", [P, TILES, K])
        w_3 = sb("w_3", [P, TILES, K])
        identb = sb("identb", [P, P], bf16)
        sel = sb("sel", [3 * M, 2 * len(PE_STEPS) + 1, P], bf16)
        relu_out = [sb(f"relu_out{l}", [P, BLK]) for l in range(3)]
        half_sum = sb("half_sum", [P, 2 * P])
        pair_sum = sb("pair_sum", [P, 3, P])
        last_sum = sb("last_sum", [P, P])
        z = sb("z", [P, 3, B])
        b_1 = sb("b_1", [P, H1 // P])
        b_2 = sb("b_2", [P, H2 // P])
        w_top3 = sb("w_top3", [P, H2 // P])
        y = x0rep[0:1, 0:B]
        w_top1 = sb("w_top1", [P, 3, H1])
        w_topd = sb("w_topd", [D, H1])
        w_top2 = sb("w_top2", [P, H1 // P, H2])
        dense = sb("dense", [D, B])
        h_1 = [prod[:, 2 * i, :, :].rearrange("p a n -> p (a n)").rearrange("p (t n) -> p t n", n=BLK)
               for i in range(2)]
        h_2 = [prod[:, 2 * i + 1, 0, :].rearrange("p (t n) -> p t n", n=BLK) for i in range(2)]
        SEL = 2 * len(PE_STEPS)
        flat = prod[:, :, :, :].rearrange("p s a n -> p (s a n)")
        sel_f32 = flat[0:3 * M, 0:(SEL + 1) * P]
        identf = flat[:, (SEL + 1) * P:(SEL + 2) * P]

        acc = [ps(f"acc{i}", [P, BLK]) for i in range(2)]
        staged = [ps(f"staged{i}", [P, BLK]) for i in range(2)]
        x1 = ps("x1", [P, HALF])
        x2 = ps("x2", [P, HALF])

        ids_in = sem("ids_in")
        consts_in = sem("consts_in")
        w1_in = sem("w1_in")
        w23_in = sem("w23_in")
        small_in = sem("small_in")
        tower_in = sem("tower_in")
        ids_padded = sem("ids_padded")
        idx_set = sem("idx_set")
        gathered = sem("gathered")
        split = sem("split")
        cast_done = sem("cast_done")
        w1_zeroed = sem("w1_zeroed")
        w1_folded = sem("w1_folded")
        filled = sem("filled")
        emptied = sem("emptied")
        scratch_in = [sem(f"scratch_in{i}") for i in range(2)]
        shift_in = sem("shift_in")
        spread_in = {s: sem(f"spread_in{s}") for s in DMA_STEPS}
        prod1_ready = sem("prod1_ready")
        prod1_free = sem("prod1_free")
        prod_ready = sem("prod_ready")
        prod_free = sem("prod_free")
        x1_ready = sem("x1_ready")
        x2_ready = sem("x2_ready")
        x2b_ready = sem("x2b_ready")
        relu_ready = [sem(f"relu_ready{l}") for l in range(3)]
        relu_free = [sem(f"relu_free{l}") for l in range(3)]
        summed = sem("summed")
        passed = sem("passed")
        h1_mm, h1_out, h2_mm, h2_out = sem("h1_mm"), sem("h1_out"), sem("h2_mm"), sem("h2_out")
        y_mm, y_out, stored = sem("y_mm"), sem("y_out"), sem("stored")

        def job_no(c, job, jobs=JOBS):
            return len(JOBS_FIRST) + len(JOBS) * c + jobs.index(job)

        def spread_done(c, q, s, jobs):
            j = 4 * PE_STEPS.index(s) + 3
            if q == 1 or j >= HEAD:
                return 2 + job_no(c, ("spread", q, j), jobs) + 1
            if isinstance(c, int) and c == 0:
                return 2 + JOBS_FIRST.index(("spread", 0, j)) + 1
            return 2 + job_no(c - 1, ("spread", 0, j)) + 1

        def x0parts_done(c, i):
            if isinstance(c, int) and c == 0:
                return 2 + JOBS_FIRST.index(("parts", i)) + 1
            return 2 + job_no(c - 1, ("parts", i)) + 1

        def products_made(stage, i):
            return (STEPS + 1) * stage + i + 1

        FIRST_SUMS, SUMS = 1, 9

        block = ctx.enter_context(nc.Block())

        @block.sync
        def _(sp):
            def held(semaphore, value):
                sp.wait_ge(semaphore, value)
                sp.sem_inc(passed, 1)

            sp.dma_start(ids_all[:, 0:CHUNKS, :], ids.rearrange("(c p) m -> p c m", p=P)).then_inc(ids_in, 16)
            sp.dma_start(identf, ident).then_inc(consts_in, 16)
            sp.dma_start(sel_f32.rearrange("p (t n) -> p t n", n=P),
                         select).then_inc(consts_in, 16)
            sp.dma_start(w_1[:, 0:4, :], w0a[:, 0:4, :]).then_inc(w1_in, 16)
            sp.dma_start(w_1[0:L1_LAST, 4, :], w0a[0:L1_LAST, 4, :]).then_inc(w1_in, 16)
            sp.wait_ge(w1_zeroed, 1)
            sp.dma_start(w_1b[M:P, 0, :], w0b[M:P, 0, :]).then_inc(w1_in, 16)
            sp.dma_start(w_1b[:, 1:4, :], w0b[:, 1:4, :]).then_inc(w1_in, 16)
            sp.dma_start(w_1b[0:L1_LAST, 4, :], w0b[0:L1_LAST, 4, :]).then_inc(w1_in, 16)
            for w_sb, w_dram in ((w_2, w1), (w_3, w2)):
                for a in range(2):
                    sp.dma_start(w_sb[K * a:K * a + K, :, :],
                                 w_dram.rearrange("(t a) h k -> a h t k", a=2)[a]).then_inc(w23_in, 16)
            sp.dma_start(b_1[:, :], bt1.rearrange("(t p) -> p t", p=P), allow_slow_non_contiguous=True).then_inc(small_in, 16)
            sp.dma_start(b_2[:, :], bt2.rearrange("(t p) -> p t", p=P), allow_slow_non_contiguous=True).then_inc(small_in, 16)
            sp.dma_start(w_top3[:, :], wt3.rearrange("(t p) o -> p (t o)", p=P), allow_slow_non_contiguous=True).then_inc(small_in, 16)

            def store_x0(c, q, done):
                held(emptied, done)
                sp.dma_start(scratch[c, :, q * HALF:(q + 1) * HALF],
                             x0rep[0:2 * M, q * HALF:(q + 1) * HALF]).then_inc(scratch_in[q], 16)

            def load_shifts(c, q, pair):
                held(scratch_in[q], 16 * (c + 1))
                if not (isinstance(pair, int) and pair == 0):
                    held(prod1_ready, L1_TILES * pair)
                for g in range(SHIFTS):
                    at = scratch[c, g, q * HALF:(q + 1) * HALF]
                    src = bass.AP(tensor=at.tensor, offset=at.offset,
                                  ap=[[COLS, M], [SHIFTS * COLS, 4], [1, HALF]])
                    sp.dma_start(x0shift[M * g:M * g + M, 0:4, :], src).then_inc(shift_in, 16)
                sp.dma_start(x0shift[0:L1_LAST, 4, :],
                             scratch[c, M // 2:M // 2 + L1_LAST, q * HALF:(q + 1) * HALF]).then_inc(shift_in, 16)

            def load_spread(c, q, steps, stage):
                held(scratch_in[q], 16 * (c + 1))
                for s in steps:
                    if stage is not None:
                        held(prod_ready, products_made(stage, s + (s == STEPS - 1)))
                    for a in range(2):
                        at = scratch[c, 4 * s + a, q * HALF:(q + 1) * HALF]
                        src = bass.AP(tensor=at.tensor, offset=at.offset,
                                      ap=[[0, K], [2 * COLS, 2], [1, HALF]])
                        sp.dma_start(spread[K * a:K * a + K, 2 * s:2 * s + 2, :], src).then_inc(spread_in[s], 16)

            def load_tower():
                for a in range(2):
                    sp.dma_start(w_top1[K * a:K * a + K, :, :],
                                 wt1[0:3 * K, :].rearrange("(l p) n -> p l n", p=K)).then_inc(tower_in, 16)
                sp.dma_start(w_topd[:, :], wt1[3 * K:3 * K + D, :]).then_inc(tower_in, 16)
                sp.dma_start(w_top2[:, :, :], wt2.rearrange("(t p) n -> p t n", p=P)).then_inc(tower_in, 16)
                sp.dma_start(dense[:, :], dense_t).then_inc(tower_in, 16)

            store_x0(0, 0, 2 + 6)
            load_shifts(0, 0, 0)
            load_spread(0, 0, DMA_STEPS, None)
            store_x0(0, 1, 2 + 8)
            load_shifts(0, 1, 1)
            load_tower()
            with sp.Fori(0, CHUNKS - 1) as c:
                load_spread(c, 1, EARLY_STEPS, 4 * c + 1)
                store_x0(c + 1, 0, 2 + job_no(c, ("x0", 1)) + 1)
                load_spread(c, 1, LATE_STEPS, 4 * c + 1)
                load_shifts(c + 1, 0, 2 * c + 2)
                store_x0(c + 1, 1, 2 + job_no(c, ("x0", 3)) + 1)
                load_shifts(c + 1, 1, 2 * c + 3)
                load_spread(c + 1, 0, DMA_STEPS, 4 * c + 3)
            load_spread(CHUNKS - 1, 1, DMA_STEPS, 4 * (CHUNKS - 1) + 1)
            sp.wait_ge(y_out, 2)
            sp.dma_start(out.rearrange("b o -> o b"), y[:, :]).then_inc(stored, 16)
            sp.wait_ge(stored, 16)

        @block.gpsimd
        def _(pool):
            def held(semaphore, value):
                pool.wait_ge(semaphore, value)
                pool.sem_inc(passed, 1)

            def set_idx(c):
                nc.gpsimd.tensor_copy(idx[:, :], ids_all[:, c, :]).then_inc(idx_set, 1)

            def gather(fields):
                for m in fields:
                    nc.gpsimd.indirect_dma_start(
                        rows[:, m * D:(m + 1) * D], None, tables[m],
                        bass.IndirectOffsetOnAxis(ap=idx[:, m:m + 1], axis=0)).then_inc(gathered, 16)

            def split_rows(c, parts_read=0, first=False):
                held(gathered, 16 * M * (c + 1))
                if not first:
                    held(filled, parts_read)
                nc.gpsimd.tensor_copy(parts[:, 0, :], rows[:, :]).then_inc(split, 1)
                pool.wait_ge(split, 4 * c + 1)
                nc.gpsimd.tensor_tensor(rest[:, :], rows[:, :], parts[:, 0, :], ALU.subtract).then_inc(split, 1)
                held(split, 4 * c + 2)
                nc.gpsimd.tensor_copy(parts[:, 1, :], rest[:, :]).then_inc(split, 1)
                pool.wait_ge(split, 4 * c + 3)
                nc.gpsimd.tensor_tensor(parts[:, 2, :], rest[:, :], parts[:, 1, :], ALU.subtract).then_inc(split, 1)

            def layer_1(c, q, x0_done):
                pair = 2 * c + q
                pool.wait_ge(emptied, x0_done)
                pool.wait_ge(shift_in, 16 * (SHIFTS + 1) * (pair + 1))
                for j in range(L1_TILES):
                    n = P if j < L1_TILES - 1 else L1_LAST
                    pool.wait_ge(prod1_free, L1_TILES * pair + j + 1)
                    nc.gpsimd.tensor_tensor(prod1[0:n, j, :], x0rep[0:n, q * HALF:(q + 1) * HALF],
                                            x0shift[0:n, j, :], ALU.mult).then_inc(prod1_ready, 1)

            def sum_d(c, q, layer, so_far):
                r = relu_out[layer]
                pair = 2 * c + q
                pool.wait_ge(summed, so_far)
                pool.wait_ge(relu_ready[layer], pair + (2 if layer == 2 else 1))
                nc.gpsimd.tensor_tensor(half_sum[:, :], r[:, 0:2 * P], r[:, 2 * P:4 * P],
                                        ALU.add).then_inc(relu_free[layer], 1)
                pool.wait_ge(relu_free[layer], pair + 2)
                to = pair_sum[:, layer, :] if q == 0 else last_sum[:, :]
                nc.gpsimd.tensor_tensor(to, half_sum[:, 0:P], half_sum[:, P:2 * P], ALU.add).then_inc(summed, 1)
                if q == 1:
                    held(summed, so_far + 1)
                    nc.gpsimd.tensor_tensor(z[:, layer, bass.ts(c, P)], pair_sum[:, layer, :],
                                            last_sum[:, :], ALU.add).then_inc(summed, 1)

            pool.sem_inc(relu_free[0], 1)
            pool.sem_inc(relu_free[1], 1)
            pool.sem_inc(relu_free[2], 1)
            nc.gpsimd.memset(ids_all[:, CHUNKS, :], 0).then_inc(ids_padded, 1)
            pool.wait_ge(ids_padded, 1)
            pool.wait_ge(ids_in, 16)
            set_idx(0)
            pool.wait_ge(idx_set, 1)
            gather(range(M))
            split_rows(0, first=True)
            set_idx(1)
            pool.wait_ge(idx_set, 2)
            pool.wait_ge(split, 4)
            gather(range(SOON + NEXT))
            layer_1(0, 1, 2 + 8)
            gather(range(SOON + NEXT, M))
            sum_d(0, 0, 0, 0)

            def chunk(c, last):
                sums = FIRST_SUMS + SUMS * c
                if not last:
                    split_rows(c + 1, parts_read=len(JOBS_FIRST) + len(JOBS) * c)
                    set_idx(c + 2)
                    held(idx_set, c + 3)
                    held(split, 4 * (c + 2))
                    gather(range(SOON))
                sum_d(c, 0, 1, sums)
                sum_d(c, 1, 0, sums + 1)
                if not last:
                    layer_1(c + 1, 0, 2 + job_no(c, ("x0", 1)) + 1)
                    gather(range(SOON, SOON + NEXT))
                sum_d(c, 0, 2, sums + 3)
                sum_d(c, 1, 1, sums + 4)
                if not last:
                    layer_1(c + 1, 1, 2 + job_no(c, ("x0", 3)) + 1)
                    sum_d(c + 1, 0, 0, sums + 6)
                    gather(range(SOON + NEXT, M))
                    sum_d(c, 1, 2, sums + 7)
                else:
                    sum_d(c, 1, 2, sums + 6)

            with pool.Fori(0, CHUNKS - 1) as c:
                chunk(c, False)
            chunk(CHUNKS - 1, True)
            pool.wait_ge(gathered, 16 * M * (CHUNKS + 1))

        @block.vector
        def _(dve):
            nc.vector.memset(w_1b[0:M, 0, :], 0.0).then_inc(w1_zeroed, 1)
            dve.wait_ge(consts_in, 32)
            nc.vector.tensor_copy(identb[:, :], identf).then_inc(cast_done, 1)
            nc.vector.tensor_copy(sel[:, :, :].rearrange("p t n -> p (t n)"), sel_f32).then_inc(cast_done, 1)
            dve.wait_ge(w1_in, 80)
            dve.wait_ge(w1_zeroed, 1)
            nc.vector.tensor_tensor(w_1[:, 0:4, :], w_1[:, 0:4, :], w_1b[:, 0:4, :], ALU.add).then_inc(w1_folded, 1)
            nc.vector.tensor_tensor(w_1[0:L1_LAST, 4, :], w_1[0:L1_LAST, 4, :], w_1b[0:L1_LAST, 4, :],
                                    ALU.add).then_inc(w1_folded, 1)
            dve.wait_ge(cast_done, 2)

            def products(n, s, x):
                dve.wait_ge(prod_free, n + 1)
                if s < STEPS - 1:
                    nc.vector.tensor_tensor(prod[:, s % SLOTS, :, :], spread[:, 2 * s:2 * s + 2, :],
                                            x[:, :].rearrange("p (a n) -> p a n", a=1).to_broadcast([P, 2, HALF]),
                                            ALU.mult).then_inc(prod_ready, 1)
                else:
                    for a in range(2):
                        nc.vector.tensor_tensor(prod[:, s % SLOTS, a, :], spread[:, 2 * s + a, :], x[:, :],
                                                ALU.mult).then_inc(prod_ready, 1)

            dve.wait_ge(emptied, 2 + 6)
            dve.wait_ge(shift_in, 16 * (SHIFTS + 1))
            for j in range(L1_TILES):
                n = P if j < L1_TILES - 1 else L1_LAST
                nc.vector.tensor_tensor(prod1[0:n, j, :], x0rep[0:n, 0:HALF], x0shift[0:n, j, :],
                                        ALU.mult).then_inc(prod1_ready, 1)

            def chunk(c, jobs):
                for q in range(2):
                    n = 4 * STEPS * c + 2 * STEPS * q
                    dve.wait_ge(x1_ready, 2 * c + q + 1)
                    for s in range(STEPS):
                        if s in DMA_STEPS:
                            dve.wait_ge(spread_in[s], 32 * (2 * c + q + 1))
                        else:
                            dve.wait_ge(emptied, spread_done(c, q, s, jobs))
                        products(n + s, s, x1)
                    dve.wait_ge(prod_free, SLOTS + n + STEPS)
                    for half in range(2):
                        nc.vector.tensor_scalar(x2[K * half:K * half + K, BLK:2 * BLK], acc[q][K:2 * K, :],
                                                0.0, None, ALU.max).then_inc(x2b_ready, 1)
                    dve.wait_ge(x2b_ready, 2 * (2 * c + q + 1))
                    dve.wait_ge(x2_ready, 2 * c + q + 1)
                    for s in range(STEPS):
                        products(n + STEPS + s, s, x2)

            with dve.Fori(0, CHUNKS - 1) as c:
                chunk(c, JOBS)
            chunk(CHUNKS - 1, JOBS_LAST)

        @block.scalar
        def _(act):
            act.sem_inc(emptied, 2)
            act.sem_inc(relu_ready[2], 1)

            def empty(n, bank, job):
                src = staged[bank % 2]
                act.wait_ge(filled, n + 1)
                if job[0] == "spread":
                    t, blk = spread_at(job[2])
                    nc.scalar.activation(spread[:, t, blk * BLK:(blk + 1) * BLK], src[:, :],
                                         ACT.Copy).then_inc(emptied, 1)
                elif job[0] == "x0":
                    i = job[1]
                    nc.scalar.activation(x0rep[:, i * QUART:(i + 1) * QUART], src[:, :],
                                         ACT.Copy).then_inc(emptied, 1)
                else:
                    i = job[1]
                    nc.scalar.activation(x0parts[:, i * QUART:(i + 1) * QUART],
                                         src[0:3 * M, 0:QUART // 2].bitcast(bf16), ACT.Copy).then_inc(emptied, 1)

            def twice(bank, to, ready, layer, pair):
                for blk in range(2 if layer == 0 else 1):
                    for half in range(2):
                        last = nc.scalar.activation(to[K * half:K * half + K, blk * BLK:(blk + 1) * BLK],
                                                    acc[bank][K * blk:K * blk + K, :], ACT.Relu)
                last.then_inc(ready, 1)
                if layer == 1:
                    act.wait_ge(x2b_ready, 2 * (pair + 1))
                once(bank, layer, pair)

            def once(bank, layer, pair):
                act.wait_ge(relu_free[layer], pair + 1)
                nc.scalar.activation(relu_out[layer][:, :], acc[bank][:, :], ACT.Relu).then_inc(relu_ready[layer], 1)

            def contracted(c, stage):
                act.wait_ge(prod_free, SLOTS + 4 * STEPS * c + STEPS * (stage + 1))

            def contracted_1(pair):
                act.wait_ge(prod1_free, L1_TILES * (pair + 2))

            for n, job in enumerate(JOBS_FIRST):
                empty(n, n, job)
            contracted_1(0)
            twice(1, x1, x1_ready, 0, 0)

            def chunk(c, plan, last):
                base, k = len(JOBS_FIRST) + len(JOBS) * c, 0

                def stage_jobs(at):
                    nonlocal k
                    for pos in sorted(at):
                        for job in at[pos]:
                            if job in (("x0", 0), ("x0", 2)):
                                q = job[1] // 2
                                act.wait_ge(prod1_ready, L1_TILES * (2 * c + q + 1))
                                act.wait_ge(scratch_in[q], 16 * (c + 1))
                            empty(base + k, len(JOBS_FIRST) + k, job)
                            k += 1

                stage_jobs(plan[0])
                contracted(c, 0)
                twice(0, x2, x2_ready, 1, 2 * c)
                contracted_1(2 * c + 1)
                twice(1, x1, x1_ready, 0, 2 * c + 1)
                stage_jobs(plan[1])
                contracted(c, 1)
                once(0, 2, 2 * c)
                stage_jobs(plan[2])
                contracted(c, 2)
                twice(1, x2, x2_ready, 1, 2 * c + 1)
                if not last:
                    contracted_1(2 * c + 2)
                    twice(0, x1, x1_ready, 0, 2 * c + 2)
                stage_jobs(plan[3])
                contracted(c, 3)
                once(0 if last else 1, 2, 2 * c + 1)

            with act.Fori(0, CHUNKS - 1) as c:
                chunk(c, PLAN, False)
            chunk(CHUNKS - 1, PLAN_LAST, True)

            act.wait_ge(small_in, 48)
            for i in range(2):
                act.wait_ge(h1_mm, i + 1)
                for t in range(H1 // P):
                    last = nc.scalar.activation(h_1[i][:, t, :], (x1, x2)[t // 2][:, (t % 2) * BLK:(t % 2 + 1) * BLK],
                                                ACT.Relu, bias=b_1[:, t:t + 1])
                last.then_inc(h1_out, 1)
                act.wait_ge(h2_mm, i + 1)
                for t in range(H2 // P):
                    last = nc.scalar.activation(h_2[i][:, t, :], acc[t][:, :], ACT.Relu, bias=b_2[:, t:t + 1])
                last.then_inc(h2_out, 1)
                act.wait_ge(y_mm, i + 1)
                nc.scalar.activation(y[:, i * BLK:(i + 1) * BLK], staged[i][0:1, :], ACT.Copy).then_inc(y_out, 1)

        @block.tensor
        def _(pe):
            pe.sem_inc(prod1_free, L1_TILES)
            pe.sem_inc(prod_free, SLOTS)

            def job_matmuls(c, n, bank, job):
                to = staged[bank % 2]
                if job == ("parts", 0):
                    pe.wait_ge(split, 4 * (c + 1))
                if job[0] == "x0":
                    pe.wait_ge(emptied, x0parts_done(c, job[1]))
                pe.wait_ge(emptied, n + 1)
                if job[0] == "spread":
                    _, q, j = job
                    col = q * HALF + (j % 2) * BLK
                    nc.tensor.matmul(to[:, :], sel[:, j // 2, :], x0parts[:, col:col + BLK],
                                     start=True, stop=True).then_inc(filled, 1)
                elif job[0] == "x0":
                    nc.tensor.matmul(to[:, :], sel[:, SEL, :], x0parts[:, job[1] * QUART:(job[1] + 1) * QUART],
                                     start=True, stop=True).then_inc(filled, 1)
                else:
                    for i in range(4):
                        d = 4 * job[1] + i
                        src = parts[:, 0, d:d + 1]
                        three = bass.AP(tensor=src.tensor, offset=src.offset,
                                        ap=[list(src.ap[0]), [D, 3 * M]])
                        last = nc.tensor.transpose(to[0:3 * M, i * P // 2:(i + 1) * P // 2].bitcast(bf16), three,
                                                   identb[:, :])
                    last.then_inc(filled, 1)

            def contract(bank, w, moving, start, stop):
                for blk in range(2):
                    last = nc.tensor.matmul(acc[bank][K * blk:K * blk + K, :], w,
                                            moving[:, blk * BLK:(blk + 1) * BLK], start=start, stop=stop)
                return last

            def layer_1(c, q, bank):
                for j in range(L1_TILES):
                    n = P if j < L1_TILES - 1 else L1_LAST
                    pe.wait_ge(prod1_ready, L1_TILES * (2 * c + q) + j + 1)
                    contract(bank, w_1[0:n, j, :], prod1[0:n, j, :], j == 0,
                             j == L1_TILES - 1).then_inc(prod1_free, 1)

            def layer(c, stage, bank, w, at, base, k):
                for i in range(TILES):
                    if i % 2 == 0:
                        pe.wait_ge(prod_ready, products_made(stage, i // 2))
                    elif i == TILES - 1:
                        pe.wait_ge(prod_ready, products_made(stage, STEPS))
                    last = contract(bank, w[:, i, :], prod[:, i // 2 % SLOTS, i % 2, :], i == 0, i == TILES - 1)
                    if i % 2 == 1:
                        last.then_inc(prod_free, 1)
                    for job in at.get(i, ()):
                        job_matmuls(c + 1, base + k, len(JOBS_FIRST) + k, job)
                        k += 1
                return k

            pe.wait_ge(consts_in, 32)
            pe.wait_ge(cast_done, 2)
            for n, job in enumerate(JOBS_FIRST):
                job_matmuls(0, n, n, job)
            pe.wait_ge(w1_folded, 2)
            layer_1(0, 0, 1)
            pe.wait_ge(w23_in, 64)

            def chunk(c, plan, last):
                base = len(JOBS_FIRST) + len(JOBS) * c
                stage = 4 * c
                pe.wait_ge(relu_ready[0], 2 * c + 1)
                k = layer(c, stage, 0, w_2, plan[0], base, 0)
                pe.wait_ge(relu_ready[2], 2 * c + 1)
                layer_1(c, 1, 1)
                pe.wait_ge(relu_ready[1], 2 * c + 1)
                k = layer(c, stage + 1, 0, w_3, plan[1], base, k)
                pe.wait_ge(relu_ready[0], 2 * c + 2)
                k = layer(c, stage + 2, 1, w_2, plan[2], base, k)
                pe.wait_ge(relu_ready[2], 2 * c + 2)
                if not last:
                    layer_1(c + 1, 0, 0)
                    pe.wait_ge(emptied, x0parts_done(c + 1, 3))
                    pe.wait_ge(relu_ready[1], 2 * c + 2)
                layer(c, stage + 3, 0 if last else 1, w_3, plan[3], base, k)

            with pe.Fori(0, CHUNKS - 1) as c:
                chunk(c, PLAN, False)
            chunk(CHUNKS - 1, PLAN_LAST, True)

            pe.wait_ge(tower_in, 80)
            pe.wait_ge(small_in, 48)
            pe.wait_ge(summed, FIRST_SUMS + SUMS * CHUNKS - 1)
            for i in range(2):
                if i:
                    pe.wait_ge(h1_out, i)
                cols = slice(i * BLK, (i + 1) * BLK)
                for t in range(H1 // P):
                    to = (x1, x2)[t // 2][:, (t % 2) * BLK:(t % 2 + 1) * BLK]
                    for l in range(3):
                        nc.tensor.matmul(to, w_top1[:, l, t * P:(t + 1) * P], z[:, l, cols],
                                         start=l == 0, stop=False)
                    last = nc.tensor.matmul(to, w_topd[:, t * P:(t + 1) * P], dense[:, cols], start=False, stop=True)
                last.then_inc(h1_mm, 1)
                pe.wait_ge(h1_out, i + 1)
                if i:
                    pe.wait_ge(h2_out, i)
                for t in range(H2 // P):
                    for s in range(H1 // P):
                        last = nc.tensor.matmul(acc[t][:, :], w_top2[:, s, t * P:(t + 1) * P], h_1[i][:, s, :],
                                                start=s == 0, stop=s == H1 // P - 1)
                last.then_inc(h2_mm, 1)
                pe.wait_ge(h2_out, i + 1)
                for s in range(H2 // P):
                    last = nc.tensor.matmul(staged[i][0:1, :], w_top3[:, s:s + 1], h_2[i][:, s, :],
                                            start=s == 0, stop=s == H2 // P - 1)
                last.then_inc(y_mm, 1)


def kernel(**inputs):
    import numpy as np
    import concourse.bacc as bacc
    from concourse.bass_utils import run_bass_kernel_spmd

    nc = bacc.Bacc("TRN2", target_bir_lowering=False, num_devices=1)
    arrays = {}

    def give(name, a):
        arrays[name] = np.ascontiguousarray(a)
        return nc.dram_tensor(name, arrays[name].shape, mybir.dt.from_np(arrays[name].dtype),
                              kind="ExternalInput").ap()

    w0 = np.asarray(inputs["L0_rec_W0"])
    g, m, j = np.meshgrid(np.arange(SHIFTS), np.arange(M), np.arange(L1_TILES), indexing="ij")
    h = (m + SHIFTS * j + g) % M
    tiles = [2 * s + a for s in PE_STEPS for a in range(2)]
    select = np.zeros((3, M, len(tiles) + 1, 2, K), np.float32)
    for i, t in enumerate(tiles):
        for a in range(2):
            select[:, 2 * t + a, i, a, :] = 1.0
    select[:, :, -1] = np.tile(np.eye(M, dtype=np.float32), (1, P // M)).reshape(M, 2, K)

    args = [give("ids", inputs["ids"]),
            [give(f"tbl_{i}", inputs[f"tbl_{i}"]) for i in range(M)],
            give("dense_t", np.asarray(inputs["dense_ctx"]).T),
            give("ident", np.eye(P, dtype=np.float32)),
            give("select", select.reshape(3 * M, len(tiles) + 1, P)),
            give("w0a", w0[m, h].reshape(P, L1_TILES, K)),
            give("w0b", w0[h, m].reshape(P, L1_TILES, K)),
            give("w1", inputs["L0_rec_W1"]), give("w2", inputs["L0_rec_W2"]),
            give("wt1", inputs["W_top1"]), give("bt1", inputs["b_top1"]),
            give("wt2", inputs["W_top2"]), give("bt2", inputs["b_top2"]),
            give("wt3", inputs["W_top3"])]
    out = nc.dram_tensor("y_out_dram", (B, 1), mybir.dt.float32, kind="ExternalOutput").ap()
    build(nc, *args, out)
    r = run_bass_kernel_spmd(nc, [arrays], core_ids=[0])
    return r.results[0]["y_out_dram"]
```

```python
import concourse.bass as bass
from concourse import mybir
from contextlib import ExitStack

B, M, D, K = 1024, 32, 16, 64
P = 128
CHUNKS = B // P
COLS = D * P
HALF = COLS // 2
BLK = HALF // 2
TILES = M * K // P
STEPS = TILES // 2
DMA_STEPS = (0, 2, 4, 5, 6)
assert 0 in DMA_STEPS and 1 not in DMA_STEPS
PE_STEPS = tuple(s for s in range(STEPS) if s not in DMA_STEPS)
SHIFTS = 4
L1_TILES = M // 2 // SHIFTS + 1
L1_LAST = M // 2
SLOTS = 4
POOL_L1 = 2
DVE_L1 = L1_TILES - POOL_L1
POOL_L2 = 3
LAYER_2 = [1, "tile 0", 2, 3, "tile 1", 4, 5, "tile 2", 6, 7]
LAYER_3 = list(range(STEPS))


def tiles_of(order):
    gpsimd = [int(s[-1]) for s in order if not isinstance(s, int)]
    out = []
    for s in order:
        if isinstance(s, int):
            out += [(t, s) for t in (2 * s, 2 * s + 1) if t not in gpsimd]
        else:
            out.append((int(s[-1]), None))
    assert sorted(t for t, _ in out) == list(range(TILES))
    return out


TILES_2, TILES_3 = tiles_of(LAYER_2), tiles_of(LAYER_3)
H1, H2 = 512, 256
QUART = COLS // 4
PORTIONS = (8, 14, 20, M)

SPREADS = 4 * len(PE_STEPS)
SEL_X0 = 2 * len(PE_STEPS)
SEL_SHIFT = SEL_X0 + 1
SELECTS = SEL_SHIFT + L1_TILES


def spread_times():
    times = []
    for j in range(SPREADS):
        s = PE_STEPS[j // 4]
        at = max([2 * s + 3] + [t + 1 for t in times[-1:]])
        assert at <= TILES + [t for t, _ in TILES_2].index(2 * s) - 2
        times.append(at)
    return times


TIMES = spread_times()
HEAD = sum(t < TILES for t in TIMES)


def head(q):
    return {TIMES[j]: [("spread", q, j)] for j in range(HEAD)}


def tail(q):
    return {TIMES[j] - TILES: [("spread", q, j)] for j in range(HEAD, SPREADS)}


def spread_at(j):
    return 2 * PE_STEPS[j // 4] + j % 4 // 2, j % 2


def with_next(at, extra):
    at = {k: list(v) for k, v in at.items()}
    for pos, job in extra:
        at.setdefault(pos, []).append(job)
    return at


NEXT_0 = (2, 3, 4, 5)
NEXT_1 = (3, 3, 4, 4)
HALF_0 = (("parts", 0), ("parts", 1), ("x0", 0), ("x0", 1))
HALF_1 = (("parts", 2), ("parts", 3), ("x0", 2), ("x0", 3))
PLAN = [tail(0),
        with_next(head(1), zip(NEXT_0, HALF_0)),
        tail(1),
        with_next(head(0), zip(NEXT_1, HALF_1))]
PLAN_LAST = [tail(0), head(1), tail(1), {}]


def in_order(plan):
    return [job for at in plan for k in sorted(at) for job in at[k]]


JOBS = in_order(PLAN)
JOBS_LAST = in_order(PLAN_LAST)
JOBS_FIRST = [*HALF_0, *HALF_1] + [("spread", 0, j) for j in range(HEAD)]
assert JOBS[-HEAD - len(HALF_1):] == JOBS_FIRST[-HEAD - len(HALF_1):]
SHIFT_AT = {4: [0, 1], 6: [2], 8: [3], 10: [4]}
GROUPS = 4
assert len(JOBS) % 2 == 0


def build(nc, ids, tables, dense_t, ident, select, w0a, w0b, w1, w2, wt1, bt1, wt2, bt2, wt3, out):
    fp32, bf16, i32 = mybir.dt.float32, mybir.dt.bfloat16, mybir.dt.int32
    ALU = mybir.AluOpType
    ACT = mybir.ActivationFunctionType

    with ExitStack() as ctx:
        def sb(name, shape, dt=fp32):
            return ctx.enter_context(nc.sbuf_tensor(name, shape, dt))

        def ps(name, shape):
            return ctx.enter_context(nc.psum_tensor(name, shape, fp32))

        def sem(name):
            return ctx.enter_context(nc.semaphore(name))

        scratch = nc.dram_tensor("x0_scratch", (CHUNKS, 2 * M, COLS), fp32, kind="Internal").ap()

        ids_all = sb("ids_all", [P, CHUNKS + 1, M], i32)
        idx = sb("idx", [P, M], i32)
        rows = sb("rows", [P, M * D])
        rest = sb("rest", [P, M * D])
        parts = sb("parts", [P, 3, M * D], bf16)
        x0rep = sb("x0rep", [P, COLS])
        x0parts = sb("x0parts", [3 * M, COLS], bf16)
        x0shift = sb("x0shift", [P, L1_TILES, HALF])
        spread = sb("spread", [P, TILES, HALF])
        prod = sb("prod", [P, SLOTS, 2, HALF])
        prod1 = sb("prod1", [P, L1_TILES, HALF])
        x1_pool = sb("x1_pool", [P, HALF])
        prod_pool = sb("prod_pool", [P, POOL_L2, HALF])
        w_1 = sb("w_1", [P, L1_TILES, K])
        w_1b = sb("w_1b", [P, L1_TILES, K])
        w_2 = sb("w_2", [P, TILES, K])
        w_3 = sb("w_3", [P, TILES, K])
        identb = sb("identb", [P, P], bf16)
        sel = sb("sel", [3 * M, SELECTS, P], bf16)
        relu_out = [sb(f"relu_out{l}", [P, BLK]) for l in range(3)]
        half_sum = sb("half_sum", [P, 2 * P])
        pair_sum = sb("pair_sum", [P, 3, P])
        last_sum = sb("last_sum", [P, P])
        z = sb("z", [P, 3, B])
        b_1 = sb("b_1", [P, H1 // P])
        b_2 = sb("b_2", [P, H2 // P])
        w_top3 = sb("w_top3", [P, H2 // P])
        y = x0rep[0:1, 0:B]
        old = [x0shift[:, :, :].rearrange("p j n -> p (j n)"), prod1[:, :, :].rearrange("p j n -> p (j n)")]
        hidden = [a[:, 0:(H1 + H2) // P * BLK].rearrange("p (t n) -> p t n", n=BLK) for a in old]
        h_1 = [a[:, 0:H1 // P, :] for a in hidden]
        h_2 = [a[:, H1 // P:(H1 + H2) // P, :] for a in hidden]
        free = (H1 + H2) // P * BLK
        top_in = old[0][:, free:free + 2 * B].rearrange("p (t n) -> p t n", n=B)
        w_top1 = old[1][:, free:free + 2 * H1].rearrange("p (t n) -> p t n", n=H1)
        w_top2 = old[1][:, free + 2 * H1:free + 2 * H1 + H1 // P * H2].rearrange("p (t n) -> p t n", n=H2)
        flat = prod[:, :, :, :].rearrange("p s a n -> p (s a n)")
        sel_f32 = flat[0:3 * M, 0:SELECTS * P]
        identf = flat[:, SELECTS * P:(SELECTS + 1) * P]

        acc = [ps(f"acc{i}", [P, BLK]) for i in range(2)]
        staged = [ps(f"staged{i}", [P, BLK]) for i in range(2)]
        x1 = ps("x1", [P, HALF])
        x2 = ps("x2", [P, HALF])
        x1_a, x1_b, x2_a, x2_b = (x[:, i * BLK:(i + 1) * BLK] for x in (x1, x2) for i in range(2))
        staged_0, staged_1 = staged[0][:, :], staged[1][:, :]
        to_h1 = [(x1_a, x1_b, staged_0, staged_1), (x2_a, x2_b, staged_0, staged_1)]
        to_h2 = [(acc[1][:, :], x1_a), (acc[0][:, :], x1_a)]
        to_y = [x1_b, staged_0]

        ids_in = sem("ids_in")
        consts_in = sem("consts_in")
        w1_in = sem("w1_in")
        w23_in = sem("w23_in")
        small_in = sem("small_in")
        tower_in = sem("tower_in")
        ids_padded = sem("ids_padded")
        idx_set = sem("idx_set")
        gathered_first = [sem(f"gathered_first{g}") for g in range(GROUPS)]
        gathered = sem("gathered")
        split_first = sem("split_first")
        split = sem("split")
        cast_done = sem("cast_done")
        w1_zeroed = sem("w1_zeroed")
        w1_folded = sem("w1_folded")
        filled = sem("filled")
        emptied = sem("emptied")
        scratch_in = [sem(f"scratch_in{i}") for i in range(2)]
        shift_in = sem("shift_in")
        spread_in = {s: sem(f"spread_in{s}") for s in DMA_STEPS}
        shifted = sem("shifted")
        prod1_ready = sem("prod1_ready")
        prod1_late = sem("prod1_late")
        prod1_free = sem("prod1_free")
        prod_ready = sem("prod_ready")
        prod_free = sem("prod_free")
        x1_ready = sem("x1_ready")
        x2_ready = sem("x2_ready")
        x1_pool_ready = sem("x1_pool_ready")
        prod_pool_ready = sem("prod_pool_ready")
        prod_pool_free = sem("prod_pool_free")
        relu_ready = [sem(f"relu_ready{l}") for l in range(3)]
        relu_free = [sem(f"relu_free{l}") for l in range(3)]
        summed = sem("summed")
        swapped = sem("swapped")
        folded = sem("folded")
        passed = sem("passed")
        h1_mm, h1_out, h2_mm, h2_out = sem("h1_mm"), sem("h1_out"), sem("h2_mm"), sem("h2_out")
        y_mm, y_out, stored = sem("y_mm"), sem("y_out"), sem("stored")

        def job_no(c, job, jobs=JOBS):
            return len(JOBS_FIRST) + len(JOBS) * c + jobs.index(job)

        def spread_done(c, q, s, jobs):
            j = 4 * PE_STEPS.index(s) + 3
            if q == 1 or j >= HEAD:
                return 2 + job_no(c, ("spread", q, j), jobs) + 1
            if isinstance(c, int) and c == 0:
                return 2 + JOBS_FIRST.index(("spread", 0, j)) + 1
            return 2 + job_no(c - 1, ("spread", 0, j)) + 1

        def x0parts_done(c, i):
            if isinstance(c, int) and c == 0:
                return 2 + JOBS_FIRST.index(("parts", i)) + 1
            return 2 + job_no(c - 1, ("parts", i)) + 1

        def products_made(pair, layer, i):
            return (2 * STEPS + 1) * pair + (STEPS if layer == 3 else 0) + i + 1

        def steps_before(pair, layer):
            return (2 * STEPS - 1) * pair + (STEPS - 1 if layer == 3 else 0)

        FIRST_SUMS, SUMS = 1, 9
        EARLY, LATE = slice(0, B - P), slice(B - P, B)

        block = ctx.enter_context(nc.Block())

        @block.sync
        def _(sp):
            def held(semaphore, value):
                sp.wait_ge(semaphore, value)
                sp.sem_inc(passed, 1)

            sp.dma_start(ids_all[:, 0:CHUNKS, :], ids.rearrange("(c p) m -> p c m", p=P)).then_inc(ids_in, 16)
            sp.dma_start(identf, ident).then_inc(consts_in, 16)
            sp.dma_start(sel_f32.rearrange("p (t n) -> p t n", n=P),
                         select).then_inc(consts_in, 16)
            sp.dma_start(w_1[:, 0:4, :], w0a[:, 0:4, :]).then_inc(w1_in, 16)
            sp.dma_start(w_1[0:L1_LAST, 4, :], w0a[0:L1_LAST, 4, :]).then_inc(w1_in, 16)
            sp.wait_ge(w1_zeroed, 1)
            sp.dma_start(w_1b[M:P, 0, :], w0b[M:P, 0, :]).then_inc(w1_in, 16)
            sp.dma_start(w_1b[:, 1:4, :], w0b[:, 1:4, :]).then_inc(w1_in, 16)
            sp.dma_start(w_1b[0:L1_LAST, 4, :], w0b[0:L1_LAST, 4, :]).then_inc(w1_in, 16)
            for w_sb, w_dram in ((w_2, w1), (w_3, w2)):
                for a in range(2):
                    sp.dma_start(w_sb[K * a:K * a + K, :, :],
                                 w_dram.rearrange("(t a) h k -> a h t k", a=2)[a]).then_inc(w23_in, 16)
            sp.dma_start(b_1[:, :], bt1.rearrange("(t p) -> p t", p=P), allow_slow_non_contiguous=True).then_inc(small_in, 16)
            sp.dma_start(b_2[:, :], bt2.rearrange("(t p) -> p t", p=P), allow_slow_non_contiguous=True).then_inc(small_in, 16)
            sp.dma_start(w_top3[:, :], wt3.rearrange("(t p) o -> p (t o)", p=P), allow_slow_non_contiguous=True).then_inc(small_in, 16)

            def store_x0(c, q, done):
                held(emptied, done)
                sp.dma_start(scratch[c, :, q * HALF:(q + 1) * HALF],
                             x0rep[0:2 * M, q * HALF:(q + 1) * HALF]).then_inc(scratch_in[q], 16)

            def load_shifts(c, q, pair):
                held(scratch_in[q], 16 * (c + 1))
                if not (isinstance(pair, int) and pair == 1):
                    held(prod1_ready, POOL_L1 * pair)
                    held(prod1_late, DVE_L1 * pair)
                for g in range(SHIFTS):
                    at = scratch[c, g, q * HALF:(q + 1) * HALF]
                    src = bass.AP(tensor=at.tensor, offset=at.offset,
                                  ap=[[COLS, M], [SHIFTS * COLS, 4], [1, HALF]])
                    sp.dma_start(x0shift[M * g:M * g + M, 0:4, :], src).then_inc(shift_in, 16)
                sp.dma_start(x0shift[0:L1_LAST, 4, :],
                             scratch[c, M // 2:M // 2 + L1_LAST, q * HALF:(q + 1) * HALF]).then_inc(shift_in, 16)

            def load_spread(c, q, steps, before):
                held(scratch_in[q], 16 * (c + 1))
                for s in steps:
                    if before is not None:
                        held(prod_ready, products_made(before, 3, s + (s == STEPS - 1)))
                    for a in range(2):
                        at = scratch[c, 4 * s + a, q * HALF:(q + 1) * HALF]
                        src = bass.AP(tensor=at.tensor, offset=at.offset,
                                      ap=[[0, K], [2 * COLS, 2], [1, HALF]])
                        sp.dma_start(spread[K * a:K * a + K, 2 * s:2 * s + 2, :], src).then_inc(spread_in[s], 16)

            def load_tower():
                sp.wait_ge(prod1_free, L1_TILES * (2 * CHUNKS + 1))
                sp.dma_start(w_top1[:, 0, :], wt1[0:P, :]).then_inc(tower_in, 16)
                sp.dma_start(w_top1[0:K + D, 1, :], wt1[P:P + K + D, :]).then_inc(tower_in, 16)
                sp.dma_start(w_top2[:, :, :], wt2.rearrange("(t p) n -> p t n", p=P)).then_inc(tower_in, 16)
                sp.dma_start(top_in[K:K + D, 1, :], dense_t).then_inc(tower_in, 16)

            store_x0(0, 0, 2 + JOBS_FIRST.index(("x0", 1)) + 1)
            load_spread(0, 0, DMA_STEPS, None)
            store_x0(0, 1, 2 + JOBS_FIRST.index(("x0", 3)) + 1)
            load_shifts(0, 1, 1)
            with sp.Fori(0, CHUNKS - 1) as c:
                load_spread(c, 1, DMA_STEPS[:2], 2 * c)
                store_x0(c + 1, 0, 2 + job_no(c, ("x0", 1)) + 1)
                load_spread(c, 1, DMA_STEPS[2:], 2 * c)
                load_shifts(c + 1, 0, 2 * c + 2)
                load_spread(c + 1, 0, DMA_STEPS[:2], 2 * c + 1)
                store_x0(c + 1, 1, 2 + job_no(c, ("x0", 3)) + 1)
                load_spread(c + 1, 0, DMA_STEPS[2:], 2 * c + 1)
                load_shifts(c + 1, 1, 2 * c + 3)
            load_spread(CHUNKS - 1, 1, DMA_STEPS, 2 * (CHUNKS - 1))
            load_tower()
            sp.wait_ge(y_out, 2)
            sp.dma_start(out.rearrange("b o -> o b"), y[:, :]).then_inc(stored, 16)
            sp.wait_ge(stored, 16)

        @block.gpsimd
        def _(pool):
            def held(semaphore, value):
                pool.wait_ge(semaphore, value)
                pool.sem_inc(passed, 1)

            def set_idx(c):
                nc.gpsimd.tensor_copy(idx[:, :], ids_all[:, c, :]).then_inc(idx_set, 1)

            def gather(fields):
                for m in fields:
                    nc.gpsimd.indirect_dma_start(
                        rows[:, m * D:(m + 1) * D], None, tables[m],
                        bass.IndirectOffsetOnAxis(ap=idx[:, m:m + 1], axis=0)).then_inc(gathered, 16)

            def gather_first(g):
                for m in range(g * M // GROUPS, (g + 1) * M // GROUPS):
                    nc.gpsimd.indirect_dma_start(
                        rows[:, m * D:(m + 1) * D], None, tables[m],
                        bass.IndirectOffsetOnAxis(ap=ids_all[:, 0, m:m + 1], axis=0)).then_inc(gathered_first[g], 16)

            def split_next(c, parts_read):
                held(gathered, 16 * M * (c + 1))
                held(filled, parts_read)
                nc.gpsimd.tensor_copy(parts[:, 0, :], rows[:, :]).then_inc(split, 1)
                pool.wait_ge(split, 4 * c + 1)
                nc.gpsimd.tensor_tensor(rest[:, :], rows[:, :], parts[:, 0, :], ALU.subtract).then_inc(split, 1)
                held(split, 4 * c + 2)
                nc.gpsimd.tensor_copy(parts[:, 1, :], rest[:, :]).then_inc(split, 1)
                pool.wait_ge(split, 4 * c + 3)
                nc.gpsimd.tensor_tensor(parts[:, 2, :], rest[:, :], parts[:, 1, :], ALU.subtract).then_inc(split, 1)

            def layer_1(pair, c, q):
                pool.wait_ge(shift_in, 16 * (SHIFTS + 1) * pair)
                for j in range(POOL_L1):
                    pool.wait_ge(prod1_free, L1_TILES * pair + j + 1)
                    nc.gpsimd.tensor_tensor(prod1[:, j, :], x0rep[:, q * HALF:(q + 1) * HALF],
                                            x0shift[:, j, :], ALU.mult).then_inc(prod1_ready, 1)

            def layer_2(pair, c, q, jobs):
                pool.wait_ge(x1_pool_ready, pair + 1)
                for t in range(POOL_L2):
                    if t == 0:
                        pool.wait_ge(spread_in[0], 32 * (pair + 1))
                    if t == 2:
                        pool.wait_ge(emptied, spread_done(c, q, 1, jobs))
                    pool.wait_ge(prod_pool_free, POOL_L2 * pair + t + 1)
                    nc.gpsimd.tensor_tensor(prod_pool[:, t, :], spread[:, t, :], x1_pool[:, :],
                                            ALU.mult).then_inc(prod_pool_ready, 1)

            def sum_d(c, q, layer, so_far):
                r = relu_out[layer]
                pair = 2 * c + q
                pool.wait_ge(summed, so_far)
                pool.wait_ge(relu_ready[layer], pair + (2 if layer == 2 else 1))
                nc.gpsimd.tensor_tensor(half_sum[:, :], r[:, 0:2 * P], r[:, 2 * P:4 * P],
                                        ALU.add).then_inc(relu_free[layer], 1)
                pool.wait_ge(relu_free[layer], pair + 2)
                to = pair_sum[:, layer, :] if q == 0 else last_sum[:, :]
                nc.gpsimd.tensor_tensor(to, half_sum[:, 0:P], half_sum[:, P:2 * P], ALU.add).then_inc(summed, 1)
                if q == 1:
                    held(summed, so_far + 1)
                    nc.gpsimd.tensor_tensor(z[:, layer, bass.ts(c, P)], pair_sum[:, layer, :],
                                            last_sum[:, :], ALU.add).then_inc(summed, 1)

            def fold(n, layer, cols, sums):
                half = layer % 2
                own = slice(K * half, K * half + K)
                held(summed, sums)
                if n:
                    held(folded, n)
                pool.wait_ge(swapped, n + 1)
                nc.gpsimd.tensor_tensor(top_in[own, layer // 2, cols], top_in[own, layer // 2, cols],
                                        z[own, layer, cols], ALU.add).then_inc(folded, 1)

            pool.sem_inc(relu_free[0], 1)
            pool.sem_inc(relu_free[1], 1)
            pool.sem_inc(relu_free[2], 1)
            pool.wait_ge(ids_in, 16)
            for g in range(GROUPS):
                gather_first(g)
            nc.gpsimd.memset(ids_all[:, CHUNKS, :], 0).then_inc(ids_padded, 1)
            set_idx(1)
            held(ids_padded, 1)
            held(idx_set, 1)
            for g in range(GROUPS):
                pool.wait_ge(split_first, 4 * (g + 1))
                gather(range(g * M // GROUPS, (g + 1) * M // GROUPS))
                if g == 2:
                    layer_2(0, 0, 0, JOBS)
            held(prod1_ready, POOL_L1)
            sum_d(0, 0, 0, 0)

            def chunk(c, last):
                sums = FIRST_SUMS + SUMS * c
                layer_1(2 * c + 1, c, 1)
                if not last:
                    split_next(c, parts_read=len(JOBS_FIRST) + len(JOBS) * c)
                    set_idx(c + 2)
                    held(idx_set, c + 2)
                    held(split, 4 * (c + 1))
                    gather(range(PORTIONS[0]))
                sum_d(c, 0, 1, sums)
                sum_d(c, 1, 0, sums + 1)
                layer_2(2 * c + 1, c, 1, JOBS_LAST if last else JOBS)
                if not last:
                    gather(range(PORTIONS[0], PORTIONS[1]))
                    layer_1(2 * c + 2, c + 1, 0)
                sum_d(c, 0, 2, sums + 3)
                if last:
                    held(gathered, 16 * M * CHUNKS)
                    for layer in range(3):
                        fold(layer, layer, EARLY, sums + 4)
                    held(folded, 3)
                sum_d(c, 1, 1, sums + 4)
                if not last:
                    gather(range(PORTIONS[1], PORTIONS[2]))
                    sum_d(c + 1, 0, 0, sums + 6)
                    layer_2(2 * c + 2, c + 1, 0, JOBS)
                    gather(range(PORTIONS[2], M))
                    sum_d(c, 1, 2, sums + 7)
                else:
                    fold(3, 0, LATE, sums + 6)
                    fold(4, 1, LATE, sums + 6)
                    held(folded, 5)
                    sum_d(c, 1, 2, sums + 6)
                    fold(5, 2, LATE, sums + 8)

            with pool.Fori(0, CHUNKS - 1) as c:
                chunk(c, False)
            chunk(CHUNKS - 1, True)

        @block.vector
        def _(dve):
            nc.vector.memset(w_1b[0:M, 0, :], 0.0).then_inc(w1_zeroed, 1)
            dve.wait_ge(consts_in, 32)
            nc.vector.tensor_copy(identb[:, :], identf).then_inc(cast_done, 1)
            nc.vector.tensor_copy(sel[:, :, :].rearrange("p t n -> p (t n)"), sel_f32).then_inc(cast_done, 1)
            dve.wait_ge(w1_in, 80)
            dve.wait_ge(w1_zeroed, 1)
            nc.vector.tensor_tensor(w_1[:, 0:4, :], w_1[:, 0:4, :], w_1b[:, 0:4, :], ALU.add).then_inc(w1_folded, 1)
            nc.vector.tensor_tensor(w_1[0:L1_LAST, 4, :], w_1[0:L1_LAST, 4, :], w_1b[0:L1_LAST, 4, :],
                                    ALU.add).then_inc(w1_folded, 1)
            dve.wait_ge(cast_done, 2)

            def products(n, s, slot, x):
                dve.wait_ge(prod_free, n + 1)
                if s == 1 and x is x1:
                    nc.vector.tensor_tensor(prod[:, slot % SLOTS, 1, :], spread[:, 2 * s + 1, :], x[:, :],
                                            ALU.mult).then_inc(prod_ready, 1)
                elif s < STEPS - 1:
                    nc.vector.tensor_tensor(prod[:, slot % SLOTS, :, :], spread[:, 2 * s:2 * s + 2, :],
                                            x[:, :].rearrange("p (a n) -> p a n", a=1).to_broadcast([P, 2, HALF]),
                                            ALU.mult).then_inc(prod_ready, 1)
                else:
                    for a in range(2):
                        nc.vector.tensor_tensor(prod[:, slot % SLOTS, a, :], spread[:, 2 * s + a, :], x[:, :],
                                                ALU.mult).then_inc(prod_ready, 1)

            def layer_1(pair, q):
                dve.wait_ge(shift_in, 16 * (SHIFTS + 1) * pair)
                for j in range(POOL_L1, L1_TILES):
                    n = P if j < L1_TILES - 1 else L1_LAST
                    dve.wait_ge(prod1_free, L1_TILES * pair + j + 1)
                    nc.vector.tensor_tensor(prod1[0:n, j, :], x0rep[0:n, q * HALF:(q + 1) * HALF],
                                            x0shift[0:n, j, :], ALU.mult).then_inc(prod1_late, 1)

            for g in range(GROUPS):
                cols = slice(g * M * D // GROUPS, (g + 1) * M * D // GROUPS)
                dve.wait_ge(gathered_first[g], 16 * M // GROUPS)
                nc.vector.tensor_copy(parts[:, 0, cols], rows[:, cols]).then_inc(split_first, 1)
                dve.wait_ge(split_first, 4 * g + 1)
                nc.vector.tensor_tensor(rest[:, cols], rows[:, cols], parts[:, 0, cols],
                                        ALU.subtract).then_inc(split_first, 1)
                dve.wait_ge(split_first, 4 * g + 2)
                nc.vector.tensor_copy(parts[:, 1, cols], rest[:, cols]).then_inc(split_first, 1)
                dve.wait_ge(split_first, 4 * g + 3)
                nc.vector.tensor_tensor(parts[:, 2, cols], rest[:, cols], parts[:, 1, cols],
                                        ALU.subtract).then_inc(split_first, 1)

            dve.wait_ge(emptied, 2 + JOBS_FIRST.index(("x0", 1)) + 1)
            for j in range(L1_TILES):
                n = P if j < L1_TILES - 1 else L1_LAST
                dve.wait_ge(shifted, j + 1)
                nc.vector.tensor_tensor(prod1[0:n, j, :], x0rep[0:n, 0:HALF], (x1, x2)[j % 2][0:n, :],
                                        ALU.mult).then_inc(prod1_ready if j < POOL_L1 else prod1_late, 1)

            def chunk(c, jobs, last):
                for q in range(2):
                    pair = 2 * c + q
                    dve.wait_ge(x1_ready, pair + 1)
                    for s in range(1, STEPS):
                        if s in DMA_STEPS:
                            dve.wait_ge(spread_in[s], 32 * (pair + 1))
                        else:
                            dve.wait_ge(emptied, spread_done(c, q, s, jobs))
                        products(steps_before(pair, 2) + s - 1, s, s - 1, x1)
                    if not (last and q == 1):
                        layer_1(pair + 1, 1 - q)
                    dve.wait_ge(x2_ready, pair + 1)
                    for s in range(STEPS):
                        products(steps_before(pair, 3) + s, s, s, x2)

            with dve.Fori(0, CHUNKS - 1) as c:
                chunk(c, JOBS, False)
            chunk(CHUNKS - 1, JOBS_LAST, True)

        @block.scalar
        def _(act):
            act.sem_inc(emptied, 2)
            act.sem_inc(relu_ready[2], 1)

            def empty(n, bank, job):
                src = staged[bank % 2]
                act.wait_ge(filled, n + 1)
                if job[0] == "spread":
                    t, blk = spread_at(job[2])
                    nc.scalar.activation(spread[:, t, blk * BLK:(blk + 1) * BLK], src[:, :],
                                         ACT.Copy).then_inc(emptied, 1)
                elif job[0] == "x0":
                    i = job[1]
                    nc.scalar.activation(x0rep[:, i * QUART:(i + 1) * QUART], src[:, :],
                                         ACT.Copy).then_inc(emptied, 1)
                else:
                    i = job[1]
                    nc.scalar.activation(x0parts[:, i * QUART:(i + 1) * QUART],
                                         src[0:3 * M, 0:QUART // 2].bitcast(bf16), ACT.Copy).then_inc(emptied, 1)

            def twice(bank, to, ready, layer, pair):
                for to, ready in ((to, ready), (x1_pool, x1_pool_ready))[:2 - layer]:
                    for blk in range(2):
                        for half in range(2):
                            last = nc.scalar.activation(to[K * half:K * half + K, blk * BLK:(blk + 1) * BLK],
                                                        acc[bank][K * blk:K * blk + K, :], ACT.Relu)
                    last.then_inc(ready, 1)
                once(bank, layer, pair)

            def once(bank, layer, pair):
                act.wait_ge(relu_free[layer], pair + 1)
                nc.scalar.activation(relu_out[layer][:, :], acc[bank][:, :], ACT.Relu).then_inc(relu_ready[layer], 1)

            def contracted(c, stage):
                before = steps_before(2 * c + stage // 2, 3) if stage % 2 == 0 else \
                    steps_before(2 * c + stage // 2 + 1, 2)
                act.wait_ge(prod_free, SLOTS + before)

            def contracted_1(pair):
                act.wait_ge(prod1_free, L1_TILES * (pair + 2))

            def swap(layer, cols, sums):
                half = layer % 2
                act.wait_ge(summed, sums)
                nc.scalar.activation(top_in[K * half:K * half + K, layer // 2, cols],
                                     z[K * (1 - half):K * (1 - half) + K, layer, cols], ACT.Copy).then_inc(swapped, 1)

            def hidden_1(i):
                for t in range(H1 // P):
                    act.wait_ge(h1_mm, H1 // P * i + t + 1)
                    nc.scalar.activation(h_1[i][:, t, :], to_h1[i][t], ACT.Relu, bias=b_1[:, t:t + 1]).then_inc(h1_out, 1)

            def hidden_2(i):
                for t in range(H2 // P):
                    act.wait_ge(h2_mm, H2 // P * i + t + 1)
                    nc.scalar.activation(h_2[i][:, t, :], to_h2[i][t], ACT.Relu, bias=b_2[:, t:t + 1]).then_inc(h2_out, 1)

            def result(i):
                act.wait_ge(y_mm, i + 1)
                nc.scalar.activation(y[:, i * BLK:(i + 1) * BLK], to_y[i][0:1, :], ACT.Copy).then_inc(y_out, 1)

            for n, job in enumerate(JOBS_FIRST):
                empty(n, n, job)
            act.wait_ge(small_in, 48)
            contracted_1(0)
            twice(1, x1, x1_ready, 0, 0)

            def chunk(c, plan, last):
                base, k = len(JOBS_FIRST) + len(JOBS) * c, 0

                def stage_jobs(at):
                    nonlocal k
                    for pos in sorted(at):
                        for job in at[pos]:
                            if job in (("x0", 0), ("x0", 2)):
                                q = job[1] // 2
                                act.wait_ge(prod1_ready, POOL_L1 * (2 * c + q + 1))
                                act.wait_ge(prod1_late, DVE_L1 * (2 * c + q + 1))
                                act.wait_ge(scratch_in[q], 16 * (c + 1))
                            empty(base + k, len(JOBS_FIRST) + k, job)
                            k += 1

                stage_jobs(plan[0])
                contracted(c, 0)
                twice(0, x2, x2_ready, 1, 2 * c)
                contracted_1(2 * c + 1)
                twice(1, x1, x1_ready, 0, 2 * c + 1)
                stage_jobs(plan[1])
                contracted(c, 1)
                once(0, 2, 2 * c)
                if last:
                    for layer in range(3):
                        swap(layer, EARLY, FIRST_SUMS + SUMS * (CHUNKS - 1))
                stage_jobs(plan[2])
                contracted(c, 2)
                twice(1, x2, x2_ready, 1, 2 * c + 1)
                if not last:
                    contracted_1(2 * c + 2)
                    twice(0, x1, x1_ready, 0, 2 * c + 2)
                else:
                    swap(0, LATE, FIRST_SUMS + SUMS * (CHUNKS - 1) + 3)
                    swap(1, LATE, FIRST_SUMS + SUMS * (CHUNKS - 1) + 6)
                    hidden_1(0)
                stage_jobs(plan[3])
                contracted(c, 3)
                once(0 if last else 1, 2, 2 * c + 1)

            with act.Fori(0, CHUNKS - 1) as c:
                chunk(c, PLAN, False)
            chunk(CHUNKS - 1, PLAN_LAST, True)

            swap(2, LATE, FIRST_SUMS + SUMS * CHUNKS - 1)
            hidden_2(0)
            hidden_1(1)
            result(0)
            hidden_2(1)
            result(1)

        @block.tensor
        def _(pe):
            pe.sem_inc(prod1_free, L1_TILES)
            pe.sem_inc(prod_free, SLOTS)
            pe.sem_inc(prod_pool_free, POOL_L2)

            def job_matmuls(c, n, bank, job):
                to = staged[bank % 2]
                if job == ("parts", 0):
                    if isinstance(c, int) and c == 0:
                        pe.wait_ge(split_first, 4 * GROUPS)
                    else:
                        pe.wait_ge(split, 4 * c)
                if job[0] == "x0":
                    pe.wait_ge(emptied, x0parts_done(c, job[1]))
                pe.wait_ge(emptied, n + 1)
                if job[0] == "spread":
                    _, q, j = job
                    col = q * HALF + (j % 2) * BLK
                    nc.tensor.matmul(to[:, :], sel[:, j // 2, :], x0parts[:, col:col + BLK],
                                     start=True, stop=True).then_inc(filled, 1)
                elif job[0] == "x0":
                    nc.tensor.matmul(to[:, :], sel[:, SEL_X0, :], x0parts[:, job[1] * QUART:(job[1] + 1) * QUART],
                                     start=True, stop=True).then_inc(filled, 1)
                else:
                    for i in range(4):
                        d = 4 * job[1] + i
                        src = parts[:, 0, d:d + 1]
                        three = bass.AP(tensor=src.tensor, offset=src.offset,
                                        ap=[list(src.ap[0]), [D, 3 * M]])
                        last = nc.tensor.transpose(to[0:3 * M, i * P // 2:(i + 1) * P // 2].bitcast(bf16), three,
                                                   identb[:, :])
                    last.then_inc(filled, 1)

            def contract(bank, w, moving, start, stop):
                for blk in range(2):
                    last = nc.tensor.matmul(acc[bank][K * blk:K * blk + K, :], w,
                                            moving[:, blk * BLK:(blk + 1) * BLK], start=start, stop=stop)
                return last

            def layer_1(c, q, bank):
                for j in range(L1_TILES):
                    n = P if j < L1_TILES - 1 else L1_LAST
                    if j < POOL_L1:
                        pe.wait_ge(prod1_ready, POOL_L1 * (2 * c + q) + j + 1)
                    else:
                        pe.wait_ge(prod1_late, DVE_L1 * (2 * c + q) + j - POOL_L1 + 1)
                    contract(bank, w_1[0:n, j, :], prod1[0:n, j, :], j == 0,
                             j == L1_TILES - 1).then_inc(prod1_free, 1)

            def layer(c, pair, number, bank, at, base, k):
                w = w_2 if number == 2 else w_3
                first = 1 if number == 2 else 0
                for i, (tile, s) in enumerate(TILES_2 if number == 2 else TILES_3):
                    if s is None:
                        pe.wait_ge(prod_pool_ready, POOL_L2 * pair + tile + 1)
                        moving = prod_pool[:, tile, :]
                    else:
                        if tile % 2 == 0 or (number == 2 and s == 1):
                            pe.wait_ge(prod_ready, products_made(pair, number, s - first))
                        elif s == STEPS - 1:
                            pe.wait_ge(prod_ready, products_made(pair, number, s - first + 1))
                        moving = prod[:, (s - first) % SLOTS, tile % 2, :]
                    last = contract(bank, w[:, tile, :], moving, i == 0, i == TILES - 1)
                    if s is None:
                        last.then_inc(prod_pool_free, 1)
                    elif tile % 2 == 1:
                        last.then_inc(prod_free, 1)
                    for job in at.get(i, ()):
                        job_matmuls(c + 1, base + k, len(JOBS_FIRST) + k, job)
                        k += 1
                return k

            pe.wait_ge(consts_in, 32)
            pe.wait_ge(cast_done, 2)
            for n, job in enumerate(JOBS_FIRST):
                for j in SHIFT_AT.get(n, ()):
                    if j >= 2:
                        pe.wait_ge(*((prod1_ready, j - 1) if j - 2 < POOL_L1 else (prod1_late, j - 1 - POOL_L1)))
                    rows_out = P if j < L1_TILES - 1 else L1_LAST
                    for blk in range(2):
                        last = nc.tensor.matmul((x1, x2)[j % 2][0:rows_out, blk * BLK:(blk + 1) * BLK],
                                                sel[:, SEL_SHIFT + j, 0:rows_out],
                                                x0parts[:, blk * BLK:(blk + 1) * BLK], start=True, stop=True)
                    last.then_inc(shifted, 1)
                job_matmuls(0, n, n, job)
            pe.wait_ge(w1_folded, 2)
            layer_1(0, 0, 1)
            pe.wait_ge(w23_in, 64)

            def tower_1(i):
                cols = slice(i * BLK, (i + 1) * BLK)
                for t in range(H1 // P):
                    nc.tensor.matmul(to_h1[i][t], w_top1[:, 0, t * P:(t + 1) * P], top_in[:, 0, cols],
                                     start=True, stop=False)
                    nc.tensor.matmul(to_h1[i][t], w_top1[0:K + D, 1, t * P:(t + 1) * P],
                                     top_in[0:K + D, 1, cols], start=False, stop=True).then_inc(h1_mm, 1)

            def tower_2(i):
                for s in range(H1 // P):
                    pe.wait_ge(h1_out, H1 // P * i + s + 1)
                    for t in range(H2 // P):
                        last = nc.tensor.matmul(to_h2[i][t], w_top2[:, s, t * P:(t + 1) * P], h_1[i][:, s, :],
                                                start=s == 0, stop=s == H1 // P - 1)
                        if s == H1 // P - 1:
                            last.then_inc(h2_mm, 1)

            def tower_3(i):
                for s in range(H2 // P):
                    pe.wait_ge(h2_out, H2 // P * i + s + 1)
                    last = nc.tensor.matmul(to_y[i][0:1, :], w_top3[:, s:s + 1], h_2[i][:, s, :],
                                            start=s == 0, stop=s == H2 // P - 1)
                last.then_inc(y_mm, 1)

            def chunk(c, plan, last):
                base = len(JOBS_FIRST) + len(JOBS) * c
                pe.wait_ge(relu_ready[0], 2 * c + 1)
                k = layer(c, 2 * c, 2, 0, plan[0], base, 0)
                pe.wait_ge(relu_ready[2], 2 * c + 1)
                layer_1(c, 1, 1)
                pe.wait_ge(relu_ready[1], 2 * c + 1)
                k = layer(c, 2 * c, 3, 0, plan[1], base, k)
                pe.wait_ge(relu_ready[0], 2 * c + 2)
                k = layer(c, 2 * c + 1, 2, 1, plan[2], base, k)
                pe.wait_ge(relu_ready[2], 2 * c + 2)
                if not last:
                    layer_1(c + 1, 0, 0)
                    pe.wait_ge(relu_ready[1], 2 * c + 2)
                else:
                    pe.wait_ge(emptied, 2 + job_no(c, JOBS_LAST[-1], JOBS_LAST) + 1)
                    pe.wait_ge(tower_in, 64)
                    pe.wait_ge(folded, 3)
                    tower_1(0)
                layer(c, 2 * c + 1, 3, 0 if last else 1, plan[3], base, k)

            with pe.Fori(0, CHUNKS - 1) as c:
                chunk(c, PLAN, False)
            chunk(CHUNKS - 1, PLAN_LAST, True)

            pe.wait_ge(small_in, 48)
            tower_2(0)
            pe.wait_ge(folded, 6)
            tower_1(1)
            tower_3(0)
            tower_2(1)
            tower_3(1)


def kernel(**inputs):
    import numpy as np
    import concourse.bacc as bacc
    from concourse.bass_utils import run_bass_kernel_spmd

    nc = bacc.Bacc("TRN2", target_bir_lowering=False, num_devices=1)
    arrays = {}

    def give(name, a):
        arrays[name] = np.ascontiguousarray(a)
        return nc.dram_tensor(name, arrays[name].shape, mybir.dt.from_np(arrays[name].dtype),
                              kind="ExternalInput").ap()

    w0 = np.asarray(inputs["L0_rec_W0"])
    g, m, j = np.meshgrid(np.arange(SHIFTS), np.arange(M), np.arange(L1_TILES), indexing="ij")
    h = (m + SHIFTS * j + g) % M
    tiles = [2 * s + a for s in PE_STEPS for a in range(2)]
    select = np.zeros((3, M, SELECTS, 2, K), np.float32)
    for i, t in enumerate(tiles):
        for a in range(2):
            select[:, 2 * t + a, i, a, :] = 1.0
    eye = np.eye(M, dtype=np.float32)
    select[:, :, SEL_X0] = np.tile(eye, (1, P // M)).reshape(M, 2, K)
    for i in range(L1_TILES):
        select[:, :, SEL_SHIFT + i] = eye[:, h[:, :, i].reshape(P)].reshape(M, 2, K)

    args = [give("ids", inputs["ids"]),
            [give(f"tbl_{i}", inputs[f"tbl_{i}"]) for i in range(M)],
            give("dense_t", np.asarray(inputs["dense_ctx"]).T),
            give("ident", np.eye(P, dtype=np.float32)),
            give("select", select.reshape(3 * M, SELECTS, P)),
            give("w0a", w0[m, h].reshape(P, L1_TILES, K)),
            give("w0b", w0[h, m].reshape(P, L1_TILES, K)),
            give("w1", inputs["L0_rec_W1"]), give("w2", inputs["L0_rec_W2"]),
            give("wt1", inputs["W_top1"]), give("bt1", inputs["b_top1"]),
            give("wt2", inputs["W_top2"]), give("bt2", inputs["b_top2"]),
            give("wt3", inputs["W_top3"])]
    out = nc.dram_tensor("y_out_dram", (B, 1), mybir.dt.float32, kind="ExternalOutput").ap()
    build(nc, *args, out)
    r = run_bass_kernel_spmd(nc, [arrays], core_ids=[0])
    return r.results[0]["y_out_dram"]
```
